# Optimizing a Trainium2 kernel written in Bass

```python
import numpy as np
import jax
import jax.numpy as jnp

def _softmax(x, axis=-1):
    return jax.nn.softmax(x, axis=axis)

def _gelu(x):
    return jax.nn.gelu(x, approximate=True)

def _silu(x):
    return jax.nn.silu(x)

def _sigmoid(x):
    return jax.nn.sigmoid(x)

def _layernorm(x, axis=-1, eps=1e-05):
    m = jnp.mean(x, axis=axis, keepdims=True)
    v = jnp.var(x, axis=axis, keepdims=True)
    return (x - m) / jnp.sqrt(v + eps)

def _scatter_add(tgt, idx, src, axis=0):
    return tgt.at[idx].add(src)

def _segment_sum(src, seg, n):
    return jax.ops.segment_sum(src, seg, n)
kernel_name = 'mk_adaln_ffn_d1_seqx_r4_a46738'

def setup_inputs(seed: int=0):
    np.random.seed(seed)
    _w = jnp.asarray

    def _rec_inputs():
        import jax
        import jax.numpy as jnp
        _rk = jax.random.key(seed)
        x = -7.109e-05 + 0.9999 * jax.random.normal(jax.random.fold_in(_rk, 1), (32, 64, 512), jnp.float32)
        _lenS = 64 - jax.random.randint(jax.random.fold_in(_rk, 7), (32,), 0, max(1, 64 // 4) + 1, jnp.int32)
        _lenS2 = 64 - jax.random.randint(jax.random.fold_in(_rk, 8), (32,), 0, max(1, 64 // 4) + 1, jnp.int32)
        itok_B_1_198 = jax.random.randint(jax.random.fold_in(_rk, 11), (32,), 1, 199, jnp.int32)
        return (x, itok_B_1_198)
    x, itok_B_1_198 = _rec_inputs()

    def _L0_cond_setup():
        import jax, jax.numpy as jnp
        import numpy as np
        B, C, T = (128, 64, 512)
        S, D = (200, 64)
        key = jax.random.key(seed)
        k1, k2, k3 = jax.random.split(key, 3)
        x = jax.random.normal(k1, (B, C, T), dtype=jnp.float32)
        conditions = jax.random.randint(k2, (B,), 0, S, dtype=jnp.int64)
        weights = jax.random.normal(k3, (S, C, D), dtype=jnp.float32) / jnp.sqrt(jnp.float32(C))
        return {'x': x, 'conditions': conditions, 'weights': weights}
    _L0_cond_all = _L0_cond_setup()
    _L0_cond_in = {k: v for k, v in _L0_cond_all.items() if k in ('weights',)}
    del _L0_cond_all

    def _L0_ffn_setup():
        import jax, jax.numpy as jnp
        import numpy as np
        B, S, D = (4, 512, 512)
        E, F, K = (8, 256, 2)
        SF = 256
        EPS = 1e-06

        def _rmsnorm(x, w, eps=EPS):
            var = jnp.mean(x * x, axis=-1, keepdims=True)
            return x * jax.lax.rsqrt(var + eps) * w
        key = jax.random.key(seed)
        ks = jax.random.split(key, 9)
        g = lambda k, shape, scale: jax.random.normal(k, shape, jnp.float32) * scale
        return {'x': g(ks[0], (B, S, D), 1.0), 'rms_weight': jnp.ones((D,), jnp.float32), 'router_w': g(ks[1], (D, E), 0.02), 'w_gate': g(ks[2], (E, D, F), 0.02), 'w_up': g(ks[3], (E, D, F), 0.02), 'w_down': g(ks[4], (E, F, D), 0.02), 'sw_gate': g(ks[5], (D, SF), 0.02), 'sw_up': g(ks[6], (D, SF), 0.02), 'sw_down': g(ks[7], (SF, D), 0.02)}
    _L0_ffn_all = _L0_ffn_setup()
    _L0_ffn_in = {k: v for k, v in _L0_ffn_all.items() if k in ('rms_weight', 'router_w', 'w_gate', 'w_up', 'w_down', 'sw_gate', 'sw_up', 'sw_down')}
    del _L0_ffn_all
    return {'x': x, 'itok_B_1_198': itok_B_1_198, 'L0_cond_weights': _L0_cond_in['weights'], 'L0_ffn_rms_weight': _L0_ffn_in['rms_weight'], 'L0_ffn_router_w': _L0_ffn_in['router_w'], 'L0_ffn_w_gate': _L0_ffn_in['w_gate'], 'L0_ffn_w_up': _L0_ffn_in['w_up'], 'L0_ffn_w_down': _L0_ffn_in['w_down'], 'L0_ffn_sw_gate': _L0_ffn_in['sw_gate'], 'L0_ffn_sw_up': _L0_ffn_in['sw_up'], 'L0_ffn_sw_down': _L0_ffn_in['sw_down']}

def reference(x, itok_B_1_198, L0_cond_weights, L0_ffn_rms_weight, L0_ffn_router_w, L0_ffn_w_gate, L0_ffn_w_up, L0_ffn_w_down, L0_ffn_sw_gate, L0_ffn_sw_up, L0_ffn_sw_down):
    import jax
    import jax.numpy as jnp

    def _L0_cond_ref(x, conditions, weights):
        import jax, jax.numpy as jnp
        import numpy as np
        B, C, T = (128, 64, 512)
        S, D = (200, 64)
        w = weights[conditions]
        return jnp.einsum('bct,bcd->bdt', x, w)

    def _L0_ffn_ref(x, rms_weight, router_w, w_gate, w_up, w_down, sw_gate, sw_up, sw_down):
        import jax, jax.numpy as jnp
        import numpy as np
        B, S, D = (4, 512, 512)
        E, F, K = (8, 256, 2)
        SF = 256
        EPS = 1e-06

        def _rmsnorm(x, w, eps=EPS):
            var = jnp.mean(x * x, axis=-1, keepdims=True)
            return x * jax.lax.rsqrt(var + eps) * w
        b, s, d = x.shape
        e = router_w.shape[1]
        h = _rmsnorm(x, rms_weight)
        ht = h.reshape(-1, d)
        t = ht.shape[0]
        logits = ht @ router_w
        probs = jax.nn.softmax(logits, axis=-1)
        topv, topi = jax.lax.top_k(probs, K)
        topv = topv / jnp.sum(topv, axis=-1, keepdims=True)
        w_dense = jnp.zeros((t, e), ht.dtype).at[jnp.arange(t)[:, None], topi].set(topv)
        g = jnp.einsum('td,edf->tef', ht, w_gate)
        u = jnp.einsum('td,edf->tef', ht, w_up)
        eo = jnp.einsum('tef,efd->ted', jax.nn.silu(g) * u, w_down)
        moe = jnp.einsum('te,ted->td', w_dense, eo)
        sh = jax.nn.silu(ht @ sw_gate) * (ht @ sw_up) @ sw_down
        return (moe + sh).reshape(b, s, d)
    x = x + _L0_ffn_ref(_L0_cond_ref(x, itok_B_1_198, L0_cond_weights), L0_ffn_rms_weight, L0_ffn_router_w, L0_ffn_w_gate, L0_ffn_w_up, L0_ffn_w_down, L0_ffn_sw_gate, L0_ffn_sw_up, L0_ffn_sw_down)
    return x

_drawn_inputs = setup_inputs


def setup_inputs(seed=0):
    import zlib

    import numpy as np

    out = dict(_drawn_inputs(seed))
    spreads = {'L0_ffn_rms_weight': (1.0, 0.6)}
    factors = {}
    for name, (base, spread) in spreads.items():
        noise = np.random.default_rng([zlib.crc32(name.encode()), seed]).standard_normal(out[name].shape)
        drawn = base * np.exp(spread * noise) if base else spread * noise
        out[name] = jnp.asarray(drawn.astype(out[name].dtype))
    for name, factor in factors.items():
        out[name] = (out[name] * factor).astype(out[name].dtype)
    return out
```

```python
from contextlib import ExitStack

import concourse.bass as bass
from concourse import mybir
from concourse.bass import IndirectOffsetOnAxis

ALU = mybir.AluOpType
ACT = mybir.ActivationFunctionType
F32 = mybir.dt.float32
F16 = mybir.dt.float16
I32 = mybir.dt.int32
U32 = mybir.dt.uint32
AX = mybir.AxisListType

P = 128
EPS = 1e-6
H_SHIFT = 11
W_SHIFT = 14
A_SHIFT = 14
EXPONENT = 0x7F800000
TINY = 1e-30
HUGE = 1e36


def adaln_moe_kernel(nc, x, cond, cond_w, rms_w, router_w, w_gate, w_up, w_down, s_gate, s_up, s_down, out):
    B, C, D = x.shape
    S = cond_w.shape[0]
    E, F = w_gate.shape[0], w_gate.shape[2]
    NE = E + 1
    NT = B * C // P
    DC, FC = D // P, F // P
    GU, DN = DC * 2 * F, FC * D
    WE = GU + DN
    N = NE * NT
    PB = P // C

    x_rows = x.rearrange("b c t -> (b c) t")
    out_rows = out.rearrange("b c t -> (b c) t")
    cond_rows = cond_w.rearrange("s c d -> (s c) d")

    with ExitStack() as ctx:
        def sb(name, shape, dt):
            return ctx.enter_context(nc.sbuf_tensor(name, shape, dt))

        def sem(name):
            return ctx.enter_context(nc.semaphore(name))

        W = sb("W", [P, NE, 2, WE], F16)
        hT = sb("hT", [P, NT, 2, D], F16)
        acc = sb("acc", [P, NT, D], F32)
        stage = sb("stage", [P, WE], F32)
        h = sb("h", [P, 2, D], F32)
        a = sb("a", [P, 2, F], F32)
        a_scaled = sb("a_scaled", [P, 2, F], F32)
        silu = sb("silu", [P, 2, F], F32)
        aT = sb("aT", [P, 2, 2, F], F16)
        cw = sb("cw", [P, NT, C], F32)
        bd = sb("bd", [P, 4, P], F32)
        ident = sb("ident", [P, P], F32)
        cond_i = sb("cond_i", [P, B], I32)
        cond_f = sb("cond_f", [P, B], F32)
        row_in_c = sb("row_in_c", [P, 1], F32)
        cond_idx = sb("cond_idx", [P, NT], U32)
        rms = sb("rms", [P, DC], F32)
        rms_max = sb("rms_max", [P, 1], F32)
        rstage = sb("rstage", [P, DC, E], F32)
        rW = sb("rW", [P, 2, DC, E], F16)
        mx = sb("mx", [P, 2], F32)
        gmx = sb("gmx", [P, 2], F32)
        pw2 = sb("pw2", [P, 2], F32)
        inv2 = sb("inv2", [P, 2], F32)
        scl = sb("scl", [P, 2], F32)
        row_scl = sb("row_scl", [P, DC], F32)
        gu_unscale = sb("gu_unscale", [P, NE], F32)
        dn_unscale = sb("dn_unscale", [P, NE], F32)
        r_unscale = sb("r_unscale", [P, 1], F32)
        ss = sb("ss", [P, NT], F32)
        var = sb("var", [P, NT], F32)
        nhalf = sb("nhalf", [P, NT], F32)
        seed = sb("seed", [P, NT], I32)
        newton = sb("newton", [P, NT], F32)
        rstd = sb("rstd", [P, NT], F32)
        logits = sb("logits", [P, NT, E], F32)
        probs = sb("probs", [P, NT, E], F32)
        pick = sb("pick", [P, NT, E], F32)
        rank = sb("rank", [P, NT, E], F32)
        first = sb("first", [P, NT, E], F32)
        second = sb("second", [P, NT, E], F32)
        red = sb("red", [P, NT], F32)
        top = sb("top", [P, 2, NT], F32)
        tsum = sb("tsum", [P, NT], F32)
        coef = sb("coef", [P, NE, NT], F32)
        amax = sb("amax", [P, 4], F32)
        q = sb("q", [P, 4], F32)
        r = sb("r", [P, 4], F32)
        c_step = sb("c_step", [P, 4], F32)

        pG = [ctx.enter_context(nc.psum_tensor(f"pG{k}", [P, D], F32)) for k in range(2)]
        pT = [ctx.enter_context(nc.psum_tensor(f"pT{k}", [P, D], F32)) for k in range(2)]
        pY = [ctx.enter_context(nc.psum_tensor(f"pY{k}", [P, D], F32)) for k in range(2)]
        pL = ctx.enter_context(nc.psum_tensor("pL", [P, NT * E], F32))
        pJ = ctx.enter_context(nc.psum_tensor("pJ", [P, D], F32))

        x_loaded = [sem(f"x_loaded{g}") for g in range(4)]
        small_loaded = sem("small_loaded")
        stage_loaded = sem("stage_loaded")
        pool_done = sem("pool_done")
        idx_ready = sem("idx_ready")
        cw_loaded = sem("cw_loaded")
        ident_ready = sem("ident_ready")
        bd_ready = sem("bd_ready")
        y_ready = sem("y_ready")
        ss_ready = sem("ss_ready")
        dve_step = sem("dve_step")
        rstd_ready = sem("rstd_ready")
        h_ready = sem("h_ready")
        hT_ready = sem("hT_ready")
        hi_ready = sem("hi_ready")
        lo_ready = sem("lo_ready")
        logits_ready = sem("logits_ready")
        max_ready = sem("max_ready")
        gmax_ready = sem("gmax_ready")
        scale_ready = sem("scale_ready")
        whi_ready = sem("whi_ready")
        wlo_ready = sem("wlo_ready")
        router_split = sem("router_split")
        exp_in = sem("exp_in")
        exp_out = sem("exp_out")
        gu_ready = sem("gu_ready")
        silu_ready = sem("silu_ready")
        a_ready = sem("a_ready")
        r_ready = sem("r_ready")
        as_ready = sem("as_ready")
        aT_ready = sem("aT_ready")
        ahi_ready = sem("ahi_ready")
        alo_ready = sem("alo_ready")
        down_ready = sem("down_ready")
        acc_done = sem("acc_done")
        coef_ready = sem("coef_ready")
        out_written = sem("out_written")

        block = ctx.enter_context(nc.Block())

        stage_gate = stage[:, 0:DC * F]
        stage_up = stage[:, DC * F:GU]
        stage_down = stage[:, GU:WE]

        @block.sync
        def _(sp):
            sp.dma_start(cond_i[:, :], cond.rearrange("(a b) -> a b", a=1).to_broadcast([P, B])).then_inc(small_loaded, 16)
            sp.dma_start(rms[:, :], rms_w.rearrange("(p c) -> p c", c=DC)).then_inc(small_loaded, 16)
            sp.dma_start(rstage[:, :, :], router_w.rearrange("(p c) e -> p c e", c=DC)).then_inc(small_loaded, 16)
            for g in range(4):
                rows = x_rows[g * 4 * P:(g + 1) * 4 * P, :].rearrange("(i p) t -> p i t", p=P)
                sp.dma_start(acc[:, 4 * g:4 * g + 4, :], rows).then_inc(x_loaded[g], 16)

            def load_expert(gate, up, down):
                sp.dma_start(stage_gate, gate.rearrange("(p c) f -> p (c f)", c=DC)).then_inc(stage_loaded, 16)
                sp.dma_start(stage_up, up.rearrange("(p c) f -> p (c f)", c=DC)).then_inc(stage_loaded, 16)
                sp.dma_start(stage_down, down.rearrange("(p c) d -> p (c d)", c=FC)).then_inc(stage_loaded, 16)

            load_expert(s_gate, s_up, s_down)
            with sp.Fori(0, E) as e:
                sp.wait_ge(wlo_ready, e + 1)
                load_expert(w_gate[e], w_up[e], w_down[e])
            with sp.Fori(0, NT) as i:
                sp.wait_ge(acc_done, i + (N - NT + 1))
                sp.dma_start(out_rows[bass.ts(i, P), :], acc[:, i, :]).then_inc(out_written, 16)
            sp.wait_ge(out_written, 16 * NT)

        @block.gpsimd
        def _(pool):
            nc.gpsimd.memset(ident[:, :], 0.0).then_inc(pool_done, 1)
            nc.gpsimd.memset(bd[:, :, :], 0.0).then_inc(pool_done, 1)
            for b in range(PB):
                pool.wait_ge(pool_done, 2 + b)
                nc.gpsimd.iota(row_in_c[b * C:(b + 1) * C, :], [[0, 1]], base=0, channel_multiplier=1,
                               allow_small_or_imprecise_dtypes=True).then_inc(pool_done, 1)
            pool.wait_ge(pool_done, 4)
            nc.gpsimd.affine_select(out=ident[:, :], in_=ident[:, :], compare_op=ALU.not_equal, fill=1.0,
                                    base=0, pattern=[[-1, P]], channel_multiplier=1).then_inc(ident_ready, 1)
            pool.wait_ge(small_loaded, 48)
            nc.gpsimd.tensor_scalar(cond_f[:, :], cond_i[:, :], 0.0, S - 1.0, ALU.max, ALU.min).then_inc(pool_done, 1)
            pool.wait_ge(pool_done, 5)
            for b in range(PB):
                if b:
                    pool.wait_ge(idx_ready, b)
                rows = slice(b * C, (b + 1) * C)
                mine = cond_f[rows, :].rearrange("p (i b) -> p b i", b=PB)[:, b, :]
                nc.gpsimd.tensor_scalar(cond_idx[rows, :], mine, float(C), row_in_c[rows, 0:1],
                                        ALU.mult, ALU.add).then_inc(idx_ready, 1)
            pool.wait_ge(idx_ready, PB)
            for i in range(NT):
                nc.gpsimd.indirect_dma_start(out=cw[:, i, :], out_offset=None, in_=cond_rows,
                                             in_offset=IndirectOffsetOnAxis(ap=cond_idx[:, i:i + 1], axis=0)
                                             ).then_inc(cw_loaded, 16)

            def reduce_max(n):
                pool.wait_ge(max_ready, n + 1)
                nc.gpsimd.partition_all_reduce(gmx[:, :], mx[:, :], P, bass.bass_isa.ReduceOp.max).then_inc(gmax_ready, 1)

            reduce_max(0)
            pool.wait_ge(cw_loaded, 16 * NT)

            def diagonal(i, k):
                for b in range(PB):
                    rows = slice(b * C, (b + 1) * C)
                    if not isinstance(i, int) or i + b > 0:
                        pool.wait_ge(bd_ready, PB * i + b)
                    nc.gpsimd.tensor_copy(bd[rows, k, b * C:(b + 1) * C], cw[rows, i, :]).then_inc(bd_ready, 1)

            for k in range(4):
                diagonal(k, k)
            with pool.Fori(1, NT // 4) as g:
                for k in range(4):
                    pool.wait_ge(y_ready, 4 * g + (k - 3))
                    diagonal(4 * g + k, k)

            for n in range(1, NE + 1):
                reduce_max(n)

        @block.vector
        def _(dve):
            v = nc.vector
            count = [0]

            def link(ins):
                count[0] += 1
                ins.then_inc(dve_step, 1)
                dve.wait_ge(dve_step, count[0])

            dve.wait_ge(small_loaded, 48)
            link(v.tensor_reduce(rms_max[:, :], rms[:, :], AX.X, ALU.max, apply_absolute_value=True))

            def weight_scale(e, unscale_gu, unscale_dn):
                v.tensor_scalar(mx[:, 0:1], mx[:, 0:1], rms_max[:, 0:1], None, ALU.mult).then_inc(max_ready, 1)
                dve.wait_ge(gmax_ready, e + 1)
                link_e(v.tensor_scalar(gmx[:, :], gmx[:, :], TINY, HUGE, ALU.max, ALU.min))
                link_e(v.tensor_scalar(pw2[:, :].bitcast(U32), gmx[:, :].bitcast(U32), EXPONENT, None, ALU.bitwise_and))
                link_e(v.reciprocal(inv2[:, :], pw2[:, :]))
                link_e(v.tensor_scalar(scl[:, :], inv2[:, :], float(2 ** W_SHIFT), None, ALU.mult))
                v.tensor_scalar(unscale_gu, pw2[:, 0:1], float(2.0 ** -(W_SHIFT + H_SHIFT)), None, ALU.mult)
                v.tensor_scalar(unscale_dn, pw2[:, 1:2], float(2.0 ** -W_SHIFT), None, ALU.mult)
                v.tensor_scalar(row_scl[:, :], rms[:, :], scl[:, 0:1], None, ALU.mult).then_inc(scale_ready, 1)

            link_e = link
            v.memset(mx[:, :], 1.0)
            link(v.memset(r[:, :], 1.0))
            link(v.tensor_reduce(mx[:, 0:1], rstage[:, :, :], AX.XY, ALU.max, apply_absolute_value=True))
            weight_scale(0, r_unscale[:, :], c_step[:, 0:1])
            dve.wait_ge(scale_ready, 1)
            dve.wait_ge(whi_ready, 1)
            for c in range(DC):
                ins = v.scalar_tensor_tensor(rW[:, 1, c, :], rstage[:, c, :], row_scl[:, c:c + 1], rW[:, 0, c, :],
                                             ALU.mult, ALU.subtract)
            ins.then_inc(router_split, 1)

            def norm_factor(i):
                dve.wait_ge(ss_ready, i + 1)
                s = slice(i, i + 1) if isinstance(i, int) else bass.ds(i, 1)
                k = float(2.0 ** (-2 * H_SHIFT))
                link(v.tensor_scalar(var[:, s], ss[:, s], k / D, k * EPS, ALU.mult, ALU.add))
                link(v.tensor_scalar(seed[:, s], var[:, s].bitcast(I32), 1, None, ALU.logical_shift_right))
                v.tensor_scalar(nhalf[:, s], var[:, s], -0.5, None, ALU.mult)
                link(v.tensor_scalar(rstd[:, s].bitcast(I32), seed[:, s], -1.0, float(0x5F3759DF), ALU.mult, ALU.add))
                for n in range(4):
                    link(v.tensor_scalar(newton[:, s], rstd[:, s], rstd[:, s], nhalf[:, s], ALU.mult, ALU.mult))
                    ins = v.scalar_tensor_tensor(rstd[:, s], newton[:, s], 1.5, rstd[:, s], ALU.add, ALU.mult)
                    if n < 3:
                        link(ins)
                ins.then_inc(rstd_ready, 1)

            def token_low(i, k):
                dve.wait_ge(hi_ready, i + 1)
                v.tensor_tensor(hT[:, i, 1, :], pT[k][:, :], hT[:, i, 0, :], ALU.subtract).then_inc(lo_ready, 1)

            norm_factor(0)
            for i in range(1, NT):
                norm_factor(i)
                token_low(i - 1, (i - 1) % 2)
            token_low(NT - 1, (NT - 1) % 2)

            def prepare(e, n):
                dve.wait_ge(stage_loaded, 48 * (n + 1))
                v.tensor_reduce(mx[:, 1:2], stage_down, AX.X, ALU.max, apply_absolute_value=True)
                link(v.tensor_reduce(mx[:, 0:1], stage[:, 0:GU], AX.X, ALU.max, apply_absolute_value=True))
                weight_scale(n + 1, gu_unscale[:, e:e + 1], dn_unscale[:, e:e + 1])
                dve.wait_ge(scale_ready, n + 2)
                dve.wait_ge(whi_ready, n + 2)
                for c in range(DC):
                    both = "p (m c f) -> p c m f"
                    ins = v.scalar_tensor_tensor(
                        W[:, e, 1, 0:GU].rearrange(both, m=2, c=DC)[:, c],
                        stage[:, 0:GU].rearrange(both, m=2, c=DC)[:, c], row_scl[:, c:c + 1],
                        W[:, e, 0, 0:GU].rearrange(both, m=2, c=DC)[:, c], ALU.mult, ALU.subtract)
                v.scalar_tensor_tensor(W[:, e, 1, GU:WE], stage_down, scl[:, 1:2], W[:, e, 0, GU:WE],
                                       ALU.mult, ALU.subtract).then_inc(wlo_ready, 1)

            for n in range(NE):
                prepare((n + E) % NE, n)
            dve.wait_ge(wlo_ready, NE)

            dve.wait_ge(logits_ready, NT)
            def wide(ap):
                return ap.rearrange("p (i o) -> p i o", o=1).to_broadcast([P, NT, E])
            link(v.tensor_scalar(logits[:, :, :], pL[:, :].rearrange("p (i e) -> p i e", e=E), r_unscale[:, 0:1], None, ALU.mult))
            link(v.tensor_reduce(red[:, :], logits[:, :, :], AX.X, ALU.max))
            v.tensor_tensor(logits[:, :, :], logits[:, :, :], wide(red[:, :]), ALU.subtract).then_inc(exp_in, 1)
            nb = 0
            for e in range(E):
                ins = v.memset(rank[:, :, e], float(E - e))
            link(ins)
            dve.wait_ge(exp_out, 1)
            link(v.tensor_reduce(red[:, :], probs[:, :, :], AX.X, ALU.add))
            link(v.reciprocal(red[:, :], red[:, :]))
            link(v.tensor_tensor(probs[:, :, :], probs[:, :, :], wide(red[:, :]), ALU.mult))
            for k, chosen in enumerate((first, second)):
                link(v.tensor_reduce(top[:, k, :], probs[:, :, :], AX.X, ALU.max))
                link(v.tensor_tensor(pick[:, :, :], probs[:, :, :], wide(top[:, k, :]), ALU.is_equal))
                link(v.tensor_tensor(pick[:, :, :], pick[:, :, :], rank[:, :, :], ALU.mult))
                link(v.tensor_reduce(red[:, :], pick[:, :, :], AX.X, ALU.max))
                link(v.tensor_tensor(chosen[:, :, :], rank[:, :, :], wide(red[:, :]), ALU.is_equal))
                if k == 0:
                    link(v.scalar_tensor_tensor(probs[:, :, :], chosen[:, :, :], -2.0, probs[:, :, :], ALU.mult, ALU.add))
            link(v.tensor_tensor(tsum[:, :], top[:, 0, :], top[:, 1, :], ALU.add))
            link(v.reciprocal(tsum[:, :], tsum[:, :]))
            link(v.tensor_tensor(top[:, 0, :], top[:, 0, :], tsum[:, :], ALU.mult))
            link(v.tensor_tensor(top[:, 1, :], top[:, 1, :], tsum[:, :], ALU.mult))
            link(v.tensor_tensor(first[:, :, :], first[:, :, :], wide(top[:, 0, :]), ALU.mult))
            link(v.tensor_tensor(second[:, :, :], second[:, :, :], wide(top[:, 1, :]), ALU.mult))
            link(v.tensor_tensor(first[:, :, :], first[:, :, :], second[:, :, :], ALU.add))
            link(v.memset(coef[:, E, :], 1.0))
            for e in range(E):
                ins = v.tensor_scalar(coef[:, e, :], first[:, :, e], dn_unscale[:, e:e + 1], None, ALU.mult)
            link(ins)
            link(v.tensor_scalar(coef[:, E, :], coef[:, E, :], dn_unscale[:, E:E + 1], None, ALU.mult))

            coef_flat = coef[:, :, :].rearrange("p e i -> p (e i)")

            def gated(n, k, f):
                e = n // NT
                dve.wait_ge(silu_ready, n + 1)
                if f >= 2:
                    dve.wait_ge(as_ready, n - 1)
                s = k % 2
                v.scalar_tensor_tensor(a[:, s, :], pG[s][:, F:2 * F], gu_unscale[:, bass.ds(e, 1)], silu[:, s, :],
                                       ALU.mult, ALU.mult).then_inc(a_ready, 1)
                dve.wait_ge(a_ready, n + 1)
                v.tensor_reduce(amax[:, k:k + 1], a[:, s, :], AX.X, ALU.max, apply_absolute_value=True).then_inc(r_ready, 1)
                dve.wait_ge(r_ready, 3 * n + 1)
                v.tensor_scalar(q[:, k:k + 1], amax[:, k:k + 1], TINY, float(2.0 ** -A_SHIFT), ALU.max, ALU.mult).then_inc(r_ready, 1)
                dve.wait_ge(r_ready, 3 * n + 2)
                v.reciprocal(r[:, k:k + 1], q[:, k:k + 1]).then_inc(r_ready, 1)

            def low(n, k):
                s = k % 2
                dve.wait_ge(ahi_ready, n + 1)
                v.tensor_tensor(aT[:, s, 1, :], pT[s][:, 0:F], aT[:, s, 0, :], ALU.subtract).then_inc(alo_ready, 1)

            def add_out(n, k, f):
                s = k % 2
                v.tensor_scalar(c_step[:, k:k + 1], q[:, k:k + 1], coef_flat[:, bass.ds(n, 1)], None, ALU.mult).then_inc(coef_ready, 1)
                dve.wait_ge(coef_ready, n + 1)
                dve.wait_ge(down_ready, n + 1)
                if f >= 1:
                    dve.wait_ge(acc_done, n)
                i = n % NT
                v.scalar_tensor_tensor(acc[:, i, :], pY[s][:, :], c_step[:, k:k + 1], acc[:, i, :],
                                       ALU.mult, ALU.add).then_inc(acc_done, 1)

            def dve_experts(n, k, f, g=True, l=True, d=True):
                if g:
                    gated(n, k, f)
                if f >= 1 and l:
                    low(n - 1, (k - 1) % 4)
                if f >= 2 and d:
                    add_out(n - 2, (k - 2) % 4, f - 2)

            for n in range(4):
                dve_experts(n, n, n)
            with dve.Fori(1, N // 4) as g:
                for k in range(4):
                    dve_experts(4 * g + k, k, 4)
            dve_experts(N, 0, 4, g=False)
            dve_experts(N + 1, 1, 4, g=False, l=False)

        @block.scalar
        def _(act):
            sc = nc.scalar
            act.wait_ge(scale_ready, 1)
            for c in range(DC):
                ins = sc.activation(rW[:, 0, c, :], rstage[:, c, :], ACT.Copy, scale=row_scl[:, c:c + 1])
            ins.then_inc(whi_ready, 1)

            def square(i, k):
                act.wait_ge(y_ready, i + 1)
                if not (isinstance(i, int) and i == 0):
                    act.wait_ge(ss_ready, i)
                sc.activation(pJ[:, :], pG[k][:, :], ACT.Square, accum_out=ss[:, bass.ds(i, 1)]).then_inc(ss_ready, 1)

            def normalise(i, k, f):
                act.wait_ge(rstd_ready, i + 1)
                if f >= 2:
                    act.wait_ge(hT_ready, i - 1)
                sc.activation(h[:, k, :], pG[k][:, :], ACT.Copy, scale=rstd[:, bass.ds(i, 1)]).then_inc(h_ready, 1)

            def token_high(i, k):
                act.wait_ge(hT_ready, i + 1)
                sc.activation(hT[:, i, 0, :], pT[k][:, :], ACT.Copy).then_inc(hi_ready, 1)

            square(0, 0)
            square(1, 1)
            normalise(0, 0, 0)
            for i in range(1, NT):
                if i + 1 < NT:
                    pass
                normalise(i, i % 2, i)
                if i + 1 < NT:
                    square(i + 1, (i + 1) % 2)
                token_high(i - 1, (i - 1) % 2)
            token_high(NT - 1, (NT - 1) % 2)

            for n in range(NE):
                e = (n + E) % NE
                act.wait_ge(scale_ready, n + 2)
                both = "p (m c f) -> p c m f"
                for c in range(DC):
                    sc.activation(W[:, e, 0, 0:GU].rearrange(both, m=2, c=DC)[:, c],
                                  stage[:, 0:GU].rearrange(both, m=2, c=DC)[:, c], ACT.Copy,
                                  scale=row_scl[:, c:c + 1])
                sc.activation(W[:, e, 0, GU:WE], stage_down, ACT.Copy, scale=scl[:, 1:2]).then_inc(whi_ready, 1)

            act.wait_ge(exp_in, 1)
            sc.activation(probs[:, :, :], logits[:, :, :], ACT.Exp).then_inc(exp_out, 1)

            def silu_gate(n, k, f):
                s = k % 2
                act.wait_ge(gu_ready, n + 1)
                if f >= 2:
                    act.wait_ge(a_ready, n - 1)
                sc.activation(silu[:, s, :], pG[s][:, 0:F], ACT.Silu, scale=gu_unscale[:, bass.ds(n // NT, 1)]).then_inc(silu_ready, 1)

            def scale_rows(n, k, f):
                s = k % 2
                act.wait_ge(r_ready, 3 * n + 3)
                if f >= 2:
                    act.wait_ge(aT_ready, n - 1)
                sc.activation(a_scaled[:, s, :], a[:, s, :], ACT.Copy, scale=r[:, k:k + 1]).then_inc(as_ready, 1)

            def high(n, k, f):
                s = k % 2
                act.wait_ge(aT_ready, n + 1)
                if f >= 2:
                    act.wait_ge(down_ready, n - 1)
                sc.activation(aT[:, s, 0, :], pT[s][:, 0:F], ACT.Copy).then_inc(ahi_ready, 1)

            def act_experts(n, k, f, g=True):
                if g:
                    silu_gate(n, k, f)
                    scale_rows(n, k, f)
                if f >= 1:
                    high(n - 1, (k - 1) % 4, f - 1)

            for n in range(4):
                act_experts(n, n, n)
            with act.Fori(1, N // 4) as g:
                for k in range(4):
                    act_experts(4 * g + k, k, 4)
            act_experts(N, 0, 4, g=False)

        @block.tensor
        def _(pe):
            t = nc.tensor
            pe.wait_ge(ident_ready, 1)

            def condition(i, k4):
                k = k4 % 2
                pe.wait_ge(bd_ready, PB * (i + 1))
                if i % 4 == 0:
                    pe.wait_ge(x_loaded[i // 4], 16)
                if i >= 2:
                    pe.wait_ge(h_ready, i - 1)
                t.matmul(pG[k][:, :], bd[:, k4, :], acc[:, i, :], start=True, stop=True).then_inc(y_ready, 1)

            def transpose_tokens(i, k):
                pe.wait_ge(h_ready, i + 1)
                if i >= 2:
                    pe.wait_ge(lo_ready, i - 1)
                chunks = h[:, k, :].rearrange("p (d c) -> p c d", c=DC)
                for c in range(DC):
                    ins = t.transpose(pT[k][:, c * P:(c + 1) * P], chunks[:, c, :], ident[:, :])
                ins.then_inc(hT_ready, 1)

            def route(i):
                pe.wait_ge(lo_ready, i + 1)
                o = pL[:, i * E:(i + 1) * E]
                for c in range(DC):
                    for m, (u, w) in enumerate(((0, 0), (0, 1), (1, 0))):
                        ins = t.matmul(o, hT[:, i, u, c * P:(c + 1) * P], rW[:, w, c, :],
                                       start=(c == 0 and m == 0), stop=(c == DC - 1 and m == 2))
                ins.then_inc(logits_ready, 1)

            condition(0, 0)
            for i in range(NT):
                if i + 1 < NT:
                    condition(i + 1, (i + 1) % 4)
                transpose_tokens(i, i % 2)
                if i >= 1:
                    if i == 1:
                        pe.wait_ge(router_split, 1)
                    route(i - 1)
            route(NT - 1)

            def gate_up(n, k, f):
                s = k % 2
                e, i = n // NT, n % NT
                if f >= 2:
                    pe.wait_ge(a_ready, n - 1)
                for c in range(DC):
                    for m, (u, w) in enumerate(((0, 0), (0, 1), (1, 0))):
                        rhs = W[:, e, w, 0:GU].rearrange("p (m c f) -> p c m f", m=2, c=DC)[:, c]
                        ins = t.matmul(pG[s][:, :].rearrange("p (m f) -> p m f", m=2), hT[:, i, u, c * P:(c + 1) * P], rhs,
                                       start=(c == 0 and m == 0), stop=(c == DC - 1 and m == 2))
                ins.then_inc(gu_ready, 1)

            def transpose_a(n, k, f):
                s = k % 2
                pe.wait_ge(as_ready, n + 1)
                if f >= 2:
                    pe.wait_ge(alo_ready, n - 1)
                chunks = a_scaled[:, s, :].rearrange("p (f c) -> p c f", c=FC)
                for c in range(FC):
                    ins = t.transpose(pT[s][:, c * P:(c + 1) * P], chunks[:, c, :], ident[:, :])
                ins.then_inc(aT_ready, 1)

            def down(n, k, f):
                s = k % 2
                e = n // NT
                pe.wait_ge(alo_ready, n + 1)
                if f >= 2:
                    pe.wait_ge(acc_done, n - 1)
                for c in range(FC):
                    for m, (u, w) in enumerate(((0, 0), (0, 1), (1, 0))):
                        ins = t.matmul(pY[s][:, :], aT[:, s, u, c * P:(c + 1) * P],
                                       W[:, e, w, GU + c * D:GU + (c + 1) * D],
                                       start=(c == 0 and m == 0), stop=(c == FC - 1 and m == 2))
                ins.then_inc(down_ready, 1)

            def pe_experts(n, k, f, g=True, l=True):
                if g:
                    gate_up(n, k, f)
                if f >= 2:
                    down(n - 2, (k - 2) % 4, f - 2)
                if f >= 1 and l:
                    transpose_a(n - 1, (k - 1) % 4, f - 1)

            pe.wait_ge(wlo_ready, NE)
            for n in range(4):
                pe_experts(n, n, n)
            with pe.Fori(1, N // 4) as g:
                for k in range(4):
                    pe_experts(4 * g + k, k, 4)
            pe_experts(N, 0, 4, g=False)
            pe_experts(N + 1, 1, 4, g=False, l=False)


_INS = ['x', 'itok_B_1_198', 'L0_cond_weights', 'L0_ffn_rms_weight', 'L0_ffn_router_w', 'L0_ffn_w_gate', 'L0_ffn_w_up',
        'L0_ffn_w_down', 'L0_ffn_sw_gate', 'L0_ffn_sw_up', 'L0_ffn_sw_down']


def kernel(**inputs):
    import numpy as _np
    import concourse.bacc as _bacc
    from concourse import mybir as _mybir
    from concourse.bass_utils import run_bass_kernel_spmd as _run

    nc = _bacc.Bacc("TRN2", target_bir_lowering=False, num_devices=1)
    arrays, args = {}, []
    for name in _INS:
        a = _np.ascontiguousarray(inputs[name])
        arrays[f"in_{name}_dram"] = a
        args.append(nc.dram_tensor(f"in_{name}_dram", a.shape, _mybir.dt.from_np(a.dtype), kind="ExternalInput").ap())
    shape = inputs['x'].shape
    args.append(nc.dram_tensor("out_dram", tuple(shape), _mybir.dt.float32, kind="ExternalOutput").ap())
    adaln_moe_kernel(nc, *args)
    r = _run(nc, [arrays], core_ids=[0])
    return r.results[0]["out_dram"]
```

```python
from contextlib import ExitStack

import concourse.bass as bass
from concourse import mybir
from concourse.bass import IndirectOffsetOnAxis

ALU = mybir.AluOpType
ACT = mybir.ActivationFunctionType
F32 = mybir.dt.float32
F16 = mybir.dt.float16
I32 = mybir.dt.int32
U32 = mybir.dt.uint32
AX = mybir.AxisListType

P = 128
EPS = 1e-6
H_SHIFT = 11
W_SHIFT = 14
A_SHIFT = 14
EXPONENT = 0x7F800000
RSQRT_SEED = 0x5F3759DF
TINY = 1e-30
HUGE = 1e36

PARTS = ((0, 0), (0, 1), (1, 0))


def adaln_moe_kernel(nc, x, cond, cond_w, rms_w, router_w, w_gate, w_up, w_down, s_gate, s_up, s_down, out):
    B, C, D = x.shape
    S = cond_w.shape[0]
    E, F = w_gate.shape[0], w_gate.shape[2]
    TOP = 2
    NE = E + 1
    NT = B * C // P
    PB = P // C
    NP = NT // 2
    DC, FC = D // P, F // P
    GU, DN = DC * 2 * F, FC * D
    WE = GU + DN
    NR = TOP * NT + E - 1
    SA = NT // 2
    R0, R1 = SA, SA + NR
    N = NT + NR
    UNROLLED = R0 + 1
    assert (N - UNROLLED) % 2 == 0 and NT % 4 == 0

    x_rows = x.rearrange("b c t -> (b c) t")
    out_rows = out.rearrange("b c t -> (b c) t")
    cond_rows = cond_w.rearrange("s c d -> (s c) d")
    h_rows = nc.dram_tensor("h_rows", (NT * P, D), F32).ap()
    y_routed = nc.dram_tensor("y_routed", (NR * P, D), F32).ap()
    y_shared = nc.dram_tensor("y_shared", (NT * P, D), F32).ap()

    with ExitStack() as ctx:
        def sb(name, shape, dt=F32):
            return ctx.enter_context(nc.sbuf_tensor(name, shape, dt))

        def psum(name):
            return ctx.enter_context(nc.psum_tensor(name, [P, D], F32))

        def sem(name):
            return ctx.enter_context(nc.semaphore(name))

        W = sb("W", [P, NE, 2, WE], F16)
        Wf = W[:, :, :, :].rearrange("p e l w -> p (e l w)").bitcast(F32)
        X_E = E - 2
        x_early = Wf[:, X_E * WE:X_E * WE + (NT - 4) * D].rearrange("p (i d) -> p i d", d=D)
        x_late = sb("x_late", [P, 4, D])
        CS = E * WE // (4 * D)
        comb = Wf[:, 0:CS * 4 * D].rearrange("p (s k d) -> p s k d", s=CS, k=4)
        stage = sb("stage", [P, 2, WE])
        h = sb("h", [P, 4, D])
        one_hot_row = h[:, :, :].rearrange("p s d -> p (s d)").bitcast(F16).rearrange("p (m s) -> p m s", s=P)
        hT32 = sb("hT32", [P, 2, D])
        rows = sb("rows", [P, 2, D])
        rowsT = sb("rowsT", [P, 2, 2, D], F16)
        a = sb("a", [P, 2, F])
        a_scaled = sb("a_scaled", [P, 2, F])
        silu = sb("silu", [P, 2, F])
        aT = sb("aT", [P, 2, 2, F], F16)
        y = sb("y", [P, 2, D])
        cw = sb("cw", [P, NT, C])
        bd = sb("bd", [P, 4, P])
        ident = sb("ident", [P, P])
        cond_i = sb("cond_i", [P, B], I32)
        cond_f = sb("cond_f", [P, B])
        row_in_c = sb("row_in_c", [P, 1])
        cond_idx = sb("cond_idx", [P, NT], U32)
        rms = sb("rms", [P, DC])
        rms_max = sb("rms_max", [P, 1])
        router_raw = sb("router_raw", [P, DC, E])
        router = sb("router", [P, DC, E])
        mx = sb("mx", [P, 2, 2])
        gmx = sb("gmx", [P, 2, 2])
        mxc = sb("mxc", [P, 2])
        pw2 = sb("pw2", [P, 2])
        inv2 = sb("inv2", [P, 2])
        scl = sb("scl", [P, 2, 2])
        row_scl = sb("row_scl", [P, 2, DC])
        unscale = sb("unscale", [P, 2, NE])
        down_scaled = sb("down_scaled", [P, DN])
        ss = sb("ss", [P, NT])
        var = sb("var", [P, 2])
        nhalf = sb("nhalf", [P, 2])
        seed = sb("seed", [P, 2], I32)
        newton = sb("newton", [P, 2])
        rstd = sb("rstd", [P, NT])
        logits = sb("logits", [P, NT, E])
        probs = sb("probs", [P, NT, E])
        pick = sb("pick", [P, NT, E])
        prefer = sb("prefer", [P, NT, E])
        chosen = sb("chosen", [P, TOP, NT, E])
        red = sb("red", [P, NT])
        top = sb("top", [P, TOP, NT])
        tsum = sb("tsum", [P, NT])
        sel = sb("sel", [P, NT, E], F16)
        before = sb("before", [P, P], F16)
        ones = sb("ones", [P, P], F16)
        tiles_i = sb("tiles_i", [P, 2, E], I32)
        tiles_f = sb("tiles_f", [P, E])
        start = sb("start", [P, E + 1])
        start_row = sb("start_row", [P, E])
        slot_e = sb("slot_e", [P, NT, E])
        slot_f = sb("slot_f", [P, TOP, NT])
        slot_i = sb("slot_i", [P, TOP, NT], I32)
        split_i = sb("split_i", [P, 2, TOP * NT], I32)
        split_f = sb("split_f", [P, 2, TOP * NT])
        iota_row = sb("iota_row", [P, P], F16)
        iota_step = sb("iota_step", [P, NR], F16)
        iota_tile = sb("iota_tile", [P, NR])
        iota_e = sb("iota_e", [P, E])
        token = sb("token", [P, NT])
        one_hot_step = sb("one_hot_step", [P, TOP * NT, NR], F16)
        step_rows = sb("step_rows", [P, N], U32)
        idx = sb("idx", [P, 2], U32)
        expert_f = sb("expert_f", [P, NR])
        expert = sb("expert", [P, N], I32)
        is_e = sb("is_e", [P, NR, E])
        by_e = sb("by_e", [P, NR, E])
        step_unscale = sb("step_unscale", [P, 2, N])
        amax = sb("amax", [P, 2])
        q = sb("q", [P, N])
        r = sb("r", [P, N])
        y_scale = sb("y_scale", [P, N])

        pG = [psum("pG0"), psum("pG1")]
        pY = [psum("pY0"), psum("pY1")]
        pH = [psum("pH0"), psum("pH1")]
        pT = [psum("pT0"), psum("pT1")]
        pC = [pG[0], pG[1], pY[0], pY[1]]
        pLogits = pT[0][:, F:F + NT * E]
        pRank = pY[1][:, 0:NT * E]
        pCount = pY[1][:, NT * E:NT * E + E]
        pRows = pY[0][:, 0:NR]
        pJunk = pT[1]

        small_loaded = sem("small_loaded")
        x_loaded = [sem(f"x_loaded{g}") for g in range(3)]
        pool_done = sem("pool_done")
        idx_ready = sem("idx_ready")
        cw_loaded = [sem(f"cw_loaded{g}") for g in range(4)]
        const_ready = sem("const_ready")
        bd_ready = sem("bd_ready")
        cond_done = sem("cond_done")
        ss_ready = sem("ss_ready")
        dve_step = sem("dve_step")
        rstd_ready = sem("rstd_ready")
        h_ready = sem("h_ready")
        h_stored = sem("h_stored")
        hT_ready = sem("hT_ready")
        hT_copied = sem("hT_copied")
        router_ready = sem("router_ready")
        routed = sem("routed")
        stage_loaded = [sem("stage_loaded0"), sem("stage_loaded1")]
        wmax_ready = sem("wmax_ready")
        wgmax_ready = sem("wgmax_ready")
        wscale_ready = sem("wscale_ready")
        whi_ready = sem("whi_ready")
        gu_lo_ready = sem("gu_lo_ready")
        dn_scaled = sem("dn_scaled")
        dn_lo_ready = sem("dn_lo_ready")
        exp_in = sem("exp_in")
        exp_out = sem("exp_out")
        sel_ready = sem("sel_ready")
        rank_ready = sem("rank_ready")
        rank_taken = sem("rank_taken")
        one_hots_ready = sem("one_hots_ready")
        inverse_ready = sem("inverse_ready")
        rows_table = sem("rows_table")
        step_tables = sem("step_tables")
        idx_copied = sem("idx_copied")
        rows_loaded = [sem("rows_loaded0"), sem("rows_loaded1")]
        gathered = [sem("gathered0"), sem("gathered1")]
        rowsT_ready = sem("rowsT_ready")
        rhi_ready = sem("rhi_ready")
        rlo_ready = sem("rlo_ready")
        gu_ready = sem("gu_ready")
        silu_ready = sem("silu_ready")
        a_ready = sem("a_ready")
        row_scales = sem("row_scales")
        as_ready = sem("as_ready")
        aT_ready = sem("aT_ready")
        ahi_ready = sem("ahi_ready")
        alo_ready = sem("alo_ready")
        down_ready = sem("down_ready")
        y_ready = sem("y_ready")
        y_stored = [sem("y_stored0"), sem("y_stored1")]
        cx_loaded = [sem(f"cx_loaded{g}") for g in range(2)]
        cs_loaded = [sem(f"cs_loaded{g}") for g in range(NT - SA + 1)]
        cy_loaded = [sem(f"cy_loaded{i}") for i in range(NT)]
        c_part = sem("c_part")
        c_done = sem("c_done")
        out_written = sem("out_written")

        block = ctx.enter_context(nc.Block())

        def stored(eng, t):
            eng.wait_ge(y_stored[t % 2], 16 * (t // 2 + 1))

        def gu_chunk(part, c):
            return part.rearrange("p (m c f) -> p c m f", m=2, c=DC)[:, c]

        @block.sync
        def _(sp):
            sp.dma_start(cond_i[:, :], cond.rearrange("(a b) -> a b", a=1).to_broadcast([P, B])).then_inc(small_loaded, 16)
            sp.dma_start(rms[:, :], rms_w.rearrange("(p c) -> p c", c=DC)).then_inc(small_loaded, 16)
            sp.dma_start(router_raw[:, :, :], router_w.rearrange("(p c) e -> p c e", c=DC)).then_inc(small_loaded, 16)

            def load_x(dst, lo, hi, s):
                sp.dma_start(dst, x_rows[lo * P:hi * P, :].rearrange("(i p) t -> p i t", p=P)).then_inc(s, 16)

            def load_expert(s, gate, up, down):
                sp.dma_start(stage[:, s, 0:DC * F], gate.rearrange("(p c) f -> p (c f)", c=DC)).then_inc(stage_loaded[s], 16)
                sp.dma_start(stage[:, s, DC * F:GU], up.rearrange("(p c) f -> p (c f)", c=DC)).then_inc(stage_loaded[s], 16)
                sp.dma_start(stage[:, s, GU:WE], down.rearrange("(p c) d -> p (c d)", c=FC)).then_inc(stage_loaded[s], 16)

            load_x(x_early[:, 0:4, :], 0, 4, x_loaded[0])
            load_expert(0, s_gate, s_up, s_down)
            load_x(x_early[:, 4:NT - 4, :], 4, NT - 4, x_loaded[1])
            load_expert(1, w_gate[0], w_up[0], w_down[0])
            load_x(x_late[:, :, :], NT - 4, NT, x_loaded[2])

            def store_h(b, m, f):
                s = 2 * (m % 2)
                sp.wait_ge(h_ready, 2 * b + 2)
                if f:
                    sp.wait_ge(h_stored, 16 * b)
                sp.dma_start(h_rows[bass.ds(b * 2 * P, 2 * P), :].rearrange("(i p) t -> p i t", p=P),
                             h[:, s:s + 2, :]).then_inc(h_stored, 16)

            def next_weights(b, m):
                sp.wait_ge(gu_lo_ready, b + 1)
                sp.wait_ge(dn_lo_ready, b + 1)
                load_expert(m % 2, w_gate[b + 1], w_up[b + 1], w_down[b + 1])

            store_h(0, 0, False)
            next_weights(0, 0)
            store_h(1, 1, True)
            next_weights(1, 1)
            for b in range(2, 6):
                store_h(b, b % 2, True)
                next_weights(b, b % 2)
            store_h(6, 0, True)
            next_weights(6, 0)
            store_h(7, 1, True)

            def load_rows(t, tile):
                sp.wait_ge(h_stored, 16 * (tile // 2 + 1))
                if t >= 2:
                    sp.wait_ge(rowsT_ready, t - 1)
                sp.dma_start(rows[:, t % 2, :], h_rows[tile * P:(tile + 1) * P, :]).then_inc(rows_loaded[t % 2], 16)

            def store_y(t, k):
                sp.wait_ge(y_ready, t + 1)
                if isinstance(t, int) and t < R0:
                    dst = y_shared[t * P:(t + 1) * P, :]
                elif isinstance(t, int) and t >= R1:
                    dst = y_shared[(t - NR) * P:(t - NR + 1) * P, :]
                else:
                    dst = y_routed[bass.ds((t - R0) * P, P), :]
                sp.dma_start(dst, y[:, k, :]).then_inc(y_stored[k], 16)

            for t in range(4):
                load_rows(t, t)
            for t in range(SA):
                store_y(t, t % 2)
                if t + 4 < SA:
                    load_rows(t + 4, t + 4)
            with sp.Fori(SA // 2, R1 // 2) as g:
                for k in range(2):
                    store_y(2 * g + k, k)
            store_y(R1 - 1, (R1 - 1) % 2)
            sp.wait_ge(down_ready, R1)
            load_x(comb[:, 0:SA, 0, :], 0, SA, cx_loaded[0])
            for t in range(SA):
                if t < 2:
                    stored(sp, SA - 2 + t)
            sp.dma_start(comb[:, 0:SA, 1, :], y_shared[0:SA * P, :].rearrange("(i p) t -> p i t", p=P)).then_inc(cs_loaded[0], 16)
            load_x(comb[:, SA:CS, 0, :], SA, CS, cx_loaded[1])

            def store_out(i):
                sp.wait_ge(c_done, i + 1)
                sp.dma_start(out_rows[i * P:(i + 1) * P, :], comb[:, i % CS, 0, :]).then_inc(out_written, 16)

            def load_shared(i):
                stored(sp, R1 + i - SA)
                sp.dma_start(comb[:, i % CS, 1, :], y_shared[i * P:(i + 1) * P, :]).then_inc(cs_loaded[1 + i - SA], 16)

            for t in range(R1, N):
                store_y(t, t % 2)
                if t > R1 and SA + t - 1 - R1 < CS:
                    load_shared(SA + t - 1 - R1)
            for i in range(NT):
                store_out(i)
                if i + CS < NT:
                    sp.wait_ge(out_written, 16 * (i + 1))
                    load_x(comb[:, i:i + 1, 0, :], i + CS, i + CS + 1, cx_loaded[1])
                    load_shared(i + CS)
            sp.wait_ge(out_written, 16 * NT)

        @block.gpsimd
        def _(pool):
            g_ = nc.gpsimd
            small = dict(allow_small_or_imprecise_dtypes=True)
            g_.memset(ident[:, :], 0.0).then_inc(pool_done, 1)
            g_.memset(before[:, :], 1.0).then_inc(pool_done, 1)
            g_.memset(bd[:, :, :], 0.0).then_inc(pool_done, 1)
            for b in range(PB):
                pool.wait_ge(pool_done, 3 + b)
                g_.iota(row_in_c[b * C:(b + 1) * C, :], [[0, 1]], base=0, channel_multiplier=1, **small).then_inc(pool_done, 1)
            pool.wait_ge(small_loaded, 48)
            pool.wait_ge(pool_done, 3 + PB)
            g_.tensor_scalar(cond_f[:, :], cond_i[:, :], 0.0, S - 1.0, ALU.max, ALU.min).then_inc(pool_done, 1)
            pool.wait_ge(pool_done, 4 + PB)
            for b in range(PB):
                if b:
                    pool.wait_ge(idx_ready, b)
                part = slice(b * C, (b + 1) * C)
                mine = cond_f[part, :].rearrange("p (i b) -> p b i", b=PB)[:, b, :]
                g_.tensor_scalar(cond_idx[part, :], mine, float(C), row_in_c[part, 0:1],
                                 ALU.mult, ALU.add).then_inc(idx_ready, 1)
            pool.wait_ge(idx_ready, PB)

            def gather_cond(g):
                for i in range(4 * g, 4 * g + 4):
                    g_.indirect_dma_start(out=cw[:, i, :], out_offset=None, in_=cond_rows,
                                          in_offset=IndirectOffsetOnAxis(ap=cond_idx[:, i:i + 1], axis=0)
                                          ).then_inc(cw_loaded[g], 16)

            gather_cond(0)
            g_.affine_select(out=ident[:, :], in_=ident[:, :], compare_op=ALU.not_equal, fill=1.0,
                             base=0, pattern=[[-1, P]], channel_multiplier=1).then_inc(const_ready, 1)
            gather_cond(1)

            def reduce_max(n, k):
                pool.wait_ge(wmax_ready, n + 1)
                g_.partition_all_reduce(gmx[:, k, :], mx[:, k, :], P, bass.bass_isa.ReduceOp.max).then_inc(wgmax_ready, 1)

            def down_low(n, k, f):
                e = E if f == 0 else n - 1
                pool.wait_ge(wscale_ready, n + 1)
                g_.tensor_scalar(down_scaled[:, :], stage[:, k, GU:WE], scl[:, k, 1:2], None, ALU.mult).then_inc(dn_scaled, 1)
                pool.wait_ge(whi_ready, n + 1)
                pool.wait_ge(dn_scaled, n + 1)
                g_.tensor_tensor(W[:, e, 1, GU:WE], down_scaled[:, :], W[:, e, 0, GU:WE], ALU.subtract).then_inc(dn_lo_ready, 1)

            reduce_max(0, 0)
            g_.affine_select(out=before[:, :], in_=before[:, :], compare_op=ALU.is_gt, fill=0.0,
                             base=0, pattern=[[1, P]], channel_multiplier=-1).then_inc(const_ready, 1)
            g_.memset(ones[:, :], 1.0).then_inc(const_ready, 1)
            g_.iota(iota_row[:, :], [[1, P]], base=0, channel_multiplier=0, **small).then_inc(const_ready, 1)
            g_.iota(iota_step[:, :], [[1, NR]], base=0, channel_multiplier=0, **small).then_inc(const_ready, 1)
            g_.iota(iota_tile[:, :], [[1, NR]], base=0, channel_multiplier=0, **small).then_inc(const_ready, 1)
            g_.iota(iota_e[:, :], [[1, E]], base=0, channel_multiplier=0, **small).then_inc(const_ready, 1)
            g_.iota(token[:, :], [[P, NT]], base=0, channel_multiplier=1, **small).then_inc(const_ready, 1)
            g_.iota(step_rows[:, R1:N].bitcast(I32), [[P, NT - SA]], base=SA * P, channel_multiplier=1).then_inc(const_ready, 1)
            g_.memset(expert[:, :], E).then_inc(const_ready, 1)
            gather_cond(2)
            gather_cond(3)

            for n in range(NE):
                down_low(n, n % 2, n)
                if n + 1 < NE:
                    reduce_max(n + 1, (n + 1) % 2)

            pool.wait_ge(rows_table, 1)

            def gather_rows(t):
                pool.wait_ge(rowsT_ready, t - 1)
                g_.indirect_dma_start(out=rows[:, t % 2, :], out_offset=None, in_=h_rows,
                                      in_offset=IndirectOffsetOnAxis(ap=step_rows[:, t:t + 1], axis=0)
                                      ).then_inc(gathered[t % 2], 16)

            pool.wait_ge(h_stored, 16 * NP)
            nxt = R0
            while nxt < R1 + 4:
                gather_rows(nxt)
                nxt += 1

            def gather_y(i):
                if i == 0:
                    pool.wait_ge(down_ready, R1)
                    for t in (R1 - 2, R1 - 1):
                        stored(pool, t)
                if i >= CS:
                    pool.wait_ge(out_written, 16 * (i - CS + 1))
                for k in range(TOP):
                    g_.indirect_dma_start(out=comb[:, i % CS, 2 + k, :], out_offset=None, in_=y_routed,
                                          in_offset=IndirectOffsetOnAxis(ap=slot_i[:, k, i:i + 1].bitcast(U32), axis=0)
                                          ).then_inc(cy_loaded[i], 16)

            for i in range(NT):
                gather_y(i)
                if i % 2 == 0 and nxt < N:
                    gather_rows(nxt)
                    nxt += 1

        @block.vector
        def _(dve):
            v = nc.vector
            at = [0, 0]

            def link(ins):
                at[1] += 1
                ins.then_inc(dve_step, 1)
                dve.wait_ge(dve_step, at[0] + at[1])

            dve.wait_ge(small_loaded, 48)
            v.tensor_reduce(rms_max[:, :], rms[:, :], AX.X, ALU.max, apply_absolute_value=True).then_inc(router_ready, 1)
            for c in range(DC):
                v.tensor_scalar(router[:, c, :], router_raw[:, c, :], rms[:, c:c + 1], None, ALU.mult).then_inc(router_ready, 1)
            dve.wait_ge(router_ready, 1)

            def weight_max(n, k, uses):
                dve.wait_ge(stage_loaded[k], 48 * uses)
                v.tensor_reduce(mx[:, k, 1:2], stage[:, k, GU:WE], AX.X, ALU.max, apply_absolute_value=True)
                link(v.tensor_reduce(mx[:, k, 0:1], stage[:, k, 0:GU], AX.X, ALU.max, apply_absolute_value=True))
                v.tensor_scalar(mx[:, k, 0:1], mx[:, k, 0:1], rms_max[:, 0:1], None, ALU.mult).then_inc(wmax_ready, 1)

            def weight_scale(n, k, e):
                dve.wait_ge(wgmax_ready, n + 1)
                link(v.tensor_scalar(mxc[:, :], gmx[:, k, :], TINY, HUGE, ALU.max, ALU.min))
                link(v.tensor_scalar(pw2[:, :].bitcast(U32), mxc[:, :].bitcast(U32), EXPONENT, None, ALU.bitwise_and))
                v.tensor_scalar(unscale[:, 0, bass.ds(e, 1)], pw2[:, 0:1], float(2.0 ** -(W_SHIFT + H_SHIFT)), None, ALU.mult)
                v.tensor_scalar(unscale[:, 1, bass.ds(e, 1)], pw2[:, 1:2], float(2.0 ** -W_SHIFT), None, ALU.mult)
                link(v.reciprocal(inv2[:, :], pw2[:, :]))
                link(v.tensor_scalar(scl[:, k, :], inv2[:, :], float(2 ** W_SHIFT), None, ALU.mult))
                v.tensor_scalar(row_scl[:, k, :], rms[:, :], scl[:, k, 0:1], None, ALU.mult).then_inc(wscale_ready, 1)

            def gate_up_low(n, k, e):
                dve.wait_ge(wscale_ready, n + 1)
                dve.wait_ge(whi_ready, n + 1)
                for c in range(DC):
                    ins = v.scalar_tensor_tensor(gu_chunk(W[:, e, 1, 0:GU], c), gu_chunk(stage[:, k, 0:GU], c),
                                                 row_scl[:, k, c:c + 1], gu_chunk(W[:, e, 0, 0:GU], c),
                                                 ALU.mult, ALU.subtract)
                ins.then_inc(gu_lo_ready, 1)

            def norm_factors(b):
                dve.wait_ge(ss_ready, 2 * b + 2)
                k = float(2.0 ** (-2 * H_SHIFT))
                f = rstd[:, bass.ds(2 * b, 2)]
                link(v.tensor_scalar(var[:, :], ss[:, bass.ds(2 * b, 2)], k / D, k * EPS, ALU.mult, ALU.add))
                v.tensor_scalar(nhalf[:, :], var[:, :], -0.5, None, ALU.mult)
                link(v.tensor_scalar(seed[:, :], var[:, :].bitcast(I32), 1, None, ALU.logical_shift_right))
                link(v.tensor_scalar(f.bitcast(I32), seed[:, :], -1.0, float(RSQRT_SEED), ALU.mult, ALU.add))
                for n in range(4):
                    link(v.tensor_tensor(newton[:, :], f, f, ALU.mult))
                    link(v.tensor_tensor(newton[:, :], newton[:, :], nhalf[:, :], ALU.mult))
                    ins = v.scalar_tensor_tensor(f, newton[:, :], 1.5, f, ALU.add, ALU.mult)
                    if n < 3:
                        link(ins)
                ins.then_inc(rstd_ready, 1)

            def copy_hT(i, k, f):
                dve.wait_ge(hT_ready, i + 1)
                if f:
                    dve.wait_ge(routed, i - 1)
                v.tensor_copy(hT32[:, k, :], pH[k][:, :]).then_inc(hT_copied, 1)

            def diagonal(i, k):
                for b in range(PB):
                    part = slice(b * C, (b + 1) * C)
                    v.tensor_copy(bd[part, k, b * C:(b + 1) * C], cw[part, i, :]).then_inc(bd_ready, 1)

            def diagonals(b, m):
                for j in range(2):
                    dve.wait_ge(cond_done, 2 * b + j + 1)
                    diagonal(2 * b + 4 + j, 2 * m + j)

            def pair(b, m, f, scale=True, factors=True, weights=True, ahead=True):
                e = E if f == 0 else b - 1
                if ahead:
                    if b < 2:
                        dve.wait_ge(cw_loaded[b + 1], 64)
                        if b:
                            dve.wait_ge(cw_loaded[3], 64)
                    diagonals(b, m % 2)
                if scale:
                    weight_scale(b, m % 2, e)
                if factors:
                    norm_factors(b + 1)
                for j in range(2):
                    copy_hT(2 * b + j, j, f)
                if scale:
                    gate_up_low(b, m % 2, e)
                if weights:
                    uses = (b + 1) // 2 + 1 if isinstance(b, int) else (b - m) // 2 + 1 + (m + 1) // 2
                    weight_max(b + 1, (m + 1) % 2, uses)

            dve.wait_ge(pool_done, 3 + PB)
            dve.wait_ge(cw_loaded[0], 64)
            for i in range(4):
                diagonal(i, i)
            weight_max(0, 0, 1)
            norm_factors(0)
            pair(0, 0, 0)
            pair(1, 1, 1)
            before_loop = at[1]
            first = 1
            per = None
            per = 2 * (PAIR_LINKS)
            at[0] = 0
            base = at[1]
            with dve.Fori(1, 3) as g:
                at[0], at[1] = (g - 1) * per + base, 0
                for m in range(2):
                    b = 2 * g + m
                    diagonals(b, m)
                    weight_scale(b, m, b - 1)
                    norm_factors(b + 1)
                    for j in range(2):
                        copy_hT(2 * b + j, j, 1)
                    gate_up_low(b, m, b - 1)
                    weight_max(b + 1, (m + 1) % 2, g + 1 + m)
                assert at[1] == per, (at, per)
            at[0], at[1] = 0, base + 2 * per
            pair(6, 0, 1, ahead=False)
            pair(7, 1, 1, scale=False, factors=False, weights=False, ahead=False)

            def rows_low(t, k, f):
                dve.wait_ge(rhi_ready, t + 1)
                v.tensor_tensor(rowsT[:, k, 1, :], pH[k][:, :], rowsT[:, k, 0, :], ALU.subtract).then_inc(rlo_ready, 1)

            def gated(t, k, f):
                dve.wait_ge(silu_ready, t + 1)
                if f >= 2:
                    dve.wait_ge(as_ready, t - 1)
                one = bass.ds(t, 1)
                v.scalar_tensor_tensor(a[:, k, :], pG[k][:, F:2 * F], step_unscale[:, 0, one], silu[:, k, :],
                                       ALU.mult, ALU.mult).then_inc(a_ready, 1)
                dve.wait_ge(a_ready, t + 1)
                v.tensor_reduce(amax[:, k:k + 1], a[:, k, :], AX.X, ALU.max, apply_absolute_value=True).then_inc(row_scales, 1)
                dve.wait_ge(row_scales, 4 * t + 1)
                v.tensor_scalar(q[:, one], amax[:, k:k + 1], TINY, float(2.0 ** -A_SHIFT), ALU.max, ALU.mult).then_inc(row_scales, 1)
                dve.wait_ge(row_scales, 4 * t + 2)
                v.reciprocal(r[:, one], q[:, one]).then_inc(row_scales, 1)
                v.tensor_tensor(y_scale[:, one], q[:, one], step_unscale[:, 1, one], ALU.mult).then_inc(row_scales, 1)

            def a_low(t, k):
                dve.wait_ge(ahi_ready, t + 1)
                v.tensor_tensor(aT[:, k, 1, :], pT[k][:, 0:F], aT[:, k, 0, :], ALU.subtract).then_inc(alo_ready, 1)

            def step(t, k, f):
                if not isinstance(t, int) or t + 1 < N:
                    rows_low(t + 1, 1 - k, f)
                if not isinstance(t, int) or t < N:
                    gated(t, k, f)
                if f >= 1:
                    a_low(t - 1, 1 - k)

            def wide(ap):
                return ap.rearrange("p (i o) -> p i o", o=1).to_broadcast([P, NT, E])

            def choose():
                dve.wait_ge(routed, NT)
                link(v.tensor_scalar(logits[:, :, :], pLogits.rearrange("p (i e) -> p i e", e=E), float(2.0 ** -H_SHIFT), None, ALU.mult))
                link(v.tensor_reduce(red[:, :], logits[:, :, :], AX.X, ALU.max))
                v.tensor_tensor(logits[:, :, :], logits[:, :, :], wide(red[:, :]), ALU.subtract).then_inc(exp_in, 1)
                for e in range(E):
                    ins = v.memset(prefer[:, :, e], float(E - e))
                dve.wait_ge(const_ready, 10)
                link(ins)
                dve.wait_ge(exp_out, 1)
                link(v.tensor_reduce(red[:, :], probs[:, :, :], AX.X, ALU.add))
                link(v.reciprocal(red[:, :], red[:, :]))
                link(v.tensor_tensor(probs[:, :, :], probs[:, :, :], wide(red[:, :]), ALU.mult))
                for k in range(TOP):
                    link(v.tensor_reduce(top[:, k, :], probs[:, :, :], AX.X, ALU.max))
                    link(v.tensor_tensor(pick[:, :, :], probs[:, :, :], wide(top[:, k, :]), ALU.is_equal))
                    link(v.tensor_tensor(pick[:, :, :], pick[:, :, :], prefer[:, :, :], ALU.mult))
                    link(v.tensor_reduce(red[:, :], pick[:, :, :], AX.X, ALU.max))
                    link(v.tensor_tensor(chosen[:, k], prefer[:, :, :], wide(red[:, :]), ALU.is_equal))
                    if k == 0:
                        link(v.scalar_tensor_tensor(probs[:, :, :], chosen[:, k], -2.0, probs[:, :, :], ALU.mult, ALU.add))
                v.tensor_tensor(sel[:, :, :], chosen[:, 0], chosen[:, 1], ALU.add).then_inc(sel_ready, 1)
                link(v.tensor_tensor(tsum[:, :], top[:, 0, :], top[:, 1, :], ALU.add))
                link(v.reciprocal(tsum[:, :], tsum[:, :]))
                for k in range(TOP):
                    link(v.tensor_tensor(top[:, k, :], top[:, k, :], tsum[:, :], ALU.mult))

            def place():
                dve.wait_ge(rank_ready, 1)
                link(v.tensor_scalar(tiles_i[:, 0, :], pCount, float(P - 1), None, ALU.add))
                link(v.tensor_scalar(tiles_i[:, 1, :], tiles_i[:, 0, :], P.bit_length() - 1, None, ALU.logical_shift_right))
                v.memset(start[:, 0:1], 0.0)
                link(v.tensor_copy(tiles_f[:, :], tiles_i[:, 1, :]))
                for e in range(E):
                    link(v.tensor_tensor(start[:, e + 1:e + 2], start[:, e:e + 1], tiles_f[:, e:e + 1], ALU.add))
                link(v.tensor_scalar(start_row[:, :], start[:, 0:E], float(P), None, ALU.mult))
                by_tile = start_row[:, :].rearrange("p (o e) -> p o e", o=1).to_broadcast([P, NT, E])
                v.tensor_tensor(slot_e[:, :, :], pRank.rearrange("p (i e) -> p i e", e=E), by_tile, ALU.add).then_inc(rank_taken, 1)
                dve.wait_ge(rank_taken, 1)
                for k in range(TOP):
                    link(v.tensor_tensor(pick[:, :, :], slot_e[:, :, :], chosen[:, k], ALU.mult))
                    link(v.tensor_reduce(slot_f[:, k, :], pick[:, :, :], AX.X, ALU.add))
                link(v.tensor_copy(slot_i[:, :, :], slot_f[:, :, :]))
                flat = slot_i[:, :, :].rearrange("p k i -> p (k i)")
                v.tensor_scalar(split_i[:, 0, :], flat, P - 1, None, ALU.bitwise_and)
                link(v.tensor_scalar(split_i[:, 1, :], flat, P.bit_length() - 1, None, ALU.logical_shift_right))
                link(v.tensor_copy(split_f[:, :, :], split_i[:, :, :]))
                dve.wait_ge(h_stored, 16 * NP)
                for m in range(TOP * NT):
                    i = m % NT
                    v.tensor_scalar(one_hot_row[:, m, :], iota_row[:, :], split_f[:, 0, m:m + 1], None, ALU.is_equal)
                    ins = v.tensor_scalar(one_hot_step[:, m, :], iota_step[:, :], split_f[:, 1, m:m + 1],
                                          token[:, i:i + 1], ALU.is_equal, ALU.mult)
                ins.then_inc(one_hots_ready, 1)

            def routed_rows():
                dve.wait_ge(inverse_ready, 1)
                v.tensor_copy(step_rows[:, R0:R1], pRows).then_inc(rows_table, 1)

            def tables():
                link(v.memset(expert_f[:, :], 0.0))
                for e in range(1, E):
                    link(v.scalar_tensor_tensor(expert_f[:, :], iota_tile[:, :], start[:, e:e + 1], expert_f[:, :],
                                                ALU.is_ge, ALU.add))
                v.tensor_copy(expert[:, R0:R1], expert_f[:, :])
                link(v.tensor_tensor(is_e[:, :, :], expert_f[:, :].rearrange("p (t o) -> p t o", o=1).to_broadcast([P, NR, E]),
                                     iota_e[:, :].rearrange("p (o e) -> p o e", o=1).to_broadcast([P, NR, E]), ALU.is_equal))
                for m in range(2):
                    link(v.tensor_tensor(by_e[:, :, :], is_e[:, :, :],
                                         unscale[:, m, 0:E].rearrange("p (o e) -> p o e", o=1).to_broadcast([P, NR, E]), ALU.mult))
                    ins = v.tensor_reduce(step_unscale[:, m, R0:R1], by_e[:, :, :], AX.X, ALU.add)
                    link(ins)
                v.memset(amax[:, :], 0.0).then_inc(step_tables, 1)

            def shared_unscale():
                for m in range(2):
                    for lo, hi in ((0, R0), (R1, N)):
                        ins = v.tensor_scalar(step_unscale[:, m, lo:hi], iota_row[:, 0:hi - lo], 0.0, unscale[:, m, E:NE],
                                              ALU.mult, ALU.add)
                        if (m, lo) != (1, R1):
                            ins
                link(ins)
                v.memset(amax[:, :], 0.0).then_inc(step_tables, 1)

            def combine(i):
                s = i % CS
                o = comb[:, s, 0, :]
                if i < SA:
                    dve.wait_ge(cx_loaded[0], 16)
                    dve.wait_ge(cs_loaded[0], 16)
                else:
                    dve.wait_ge(cx_loaded[1], 16 if i < CS else 16 * (i - CS + 2))
                    dve.wait_ge(cs_loaded[1 + i - SA], 16)
                dve.wait_ge(cy_loaded[i], 32)
                v.scalar_tensor_tensor(o, comb[:, s, 2, :], top[:, 0, i:i + 1], o, ALU.mult, ALU.add).then_inc(c_part, 1)
                dve.wait_ge(c_part, 2 * i + 1)
                v.scalar_tensor_tensor(o, comb[:, s, 3, :], top[:, 1, i:i + 1], o, ALU.mult, ALU.add).then_inc(c_part, 1)
                dve.wait_ge(c_part, 2 * i + 2)
                v.tensor_tensor(o, o, comb[:, s, 1, :], ALU.add).then_inc(c_done, 1)

            shared_unscale()
            rows_low(0, 0, 0)
            choose()
            step(0, 0, 0)
            weight_scale(7, 1, 6)
            step(1, 1, 1)
            place()
            step(2, 0, 2)
            gate_up_low(7, 1, 6)
            weight_max(8, 0, 5)
            step(3, 1, 2)
            routed_rows()
            weight_scale(8, 0, 7)
            step(4, 0, 2)
            step(5, 1, 2)
            gate_up_low(8, 0, 7)
            tables()
            for t in range(6, UNROLLED):
                step(t, t % 2, 2)
            c_from = R1 + 3
            loops = (c_from - UNROLLED) // 2
            with dve.Fori(0, loops) as g:
                for j in range(2):
                    step(2 * g + (UNROLLED + j), (UNROLLED + j) % 2, 2)
            c = 0
            for t in range(UNROLLED + 2 * loops, N + 1):
                step(t, t % 2, 2)
                for _ in range(2):
                    combine(c)
                    c += 1
            while c < NT:
                combine(c)
                c += 1

        @block.scalar
        def _(act):
            sc = nc.scalar

            def square(i, k):
                act.wait_ge(cond_done, i + 1)
                if not isinstance(i, int) or i > 0:
                    act.wait_ge(ss_ready, i)
                sc.activation(pJunk[:, :], pC[k][:, :], ACT.Square, accum_out=ss[:, bass.ds(i, 1)]).then_inc(ss_ready, 1)

            def normalise(i, b, k, f):
                act.wait_ge(rstd_ready, b + 1)
                if f >= 2:
                    act.wait_ge(hT_ready, i - 3)
                    act.wait_ge(h_stored, 16 * (b - 1))
                sc.activation(h[:, k, :], pC[k][:, :], ACT.Copy, scale=rstd[:, bass.ds(i, 1)]).then_inc(h_ready, 1)

            def high(n, k, e):
                act.wait_ge(wscale_ready, n + 1)
                for c in range(DC):
                    sc.activation(gu_chunk(W[:, e, 0, 0:GU], c), gu_chunk(stage[:, k, 0:GU], c), ACT.Copy,
                                  scale=row_scl[:, k, c:c + 1])
                sc.activation(W[:, e, 0, GU:WE], stage[:, k, GU:WE], ACT.Copy, scale=scl[:, k, 1:2]).then_inc(whi_ready, 1)

            def pair(b, m, f, squares=True, weights=True):
                e = E if f == 0 else b - 1
                if squares:
                    for j in range(2):
                        square(2 * b + 2 + j, (2 * m + 2 + j) % 4)
                for j in range(2):
                    normalise(2 * b + j, b, (2 * m + j) % 4, f)
                if weights:
                    high(b, m % 2, e)

            square(0, 0)
            square(1, 1)
            pair(0, 0, 0)
            pair(1, 1, 1)
            with act.Fori(1, 3) as g:
                for m in range(2):
                    pair(2 * g + m, m, 2)
            pair(6, 0, 2)
            pair(7, 1, 2, squares=False, weights=False)

            def rows_high(t, k, f):
                act.wait_ge(rowsT_ready, t + 1)
                if f >= 1:
                    act.wait_ge(gu_ready, t - 1)
                sc.activation(rowsT[:, k, 0, :], pH[k][:, :], ACT.Copy).then_inc(rhi_ready, 1)

            def silu_gate(t, k, f):
                act.wait_ge(gu_ready, t + 1)
                if f >= 2:
                    act.wait_ge(a_ready, t - 1)
                sc.activation(silu[:, k, :], pG[k][:, 0:F], ACT.Silu, scale=step_unscale[:, 0, bass.ds(t, 1)]).then_inc(silu_ready, 1)

            def scale_rows(t, k, f):
                act.wait_ge(row_scales, 4 * t + 3)
                if f >= 2:
                    act.wait_ge(aT_ready, t - 1)
                sc.activation(a_scaled[:, k, :], a[:, k, :], ACT.Copy, scale=r[:, bass.ds(t, 1)]).then_inc(as_ready, 1)

            def a_high(t, k, f):
                act.wait_ge(aT_ready, t + 1)
                if f >= 2:
                    act.wait_ge(down_ready, t - 1)
                sc.activation(aT[:, k, 0, :], pT[k][:, 0:F], ACT.Copy).then_inc(ahi_ready, 1)

            def take_y(t, k, f):
                act.wait_ge(down_ready, t + 1)
                act.wait_ge(row_scales, 4 * t + 4)
                if f >= 2:
                    act.wait_ge(y_stored[k], 16 * ((t - k) // 2) if isinstance(t, int) else 8 * (t - k))
                sc.activation(y[:, k, :], pY[k][:, :], ACT.Copy, scale=y_scale[:, bass.ds(t, 1)]).then_inc(y_ready, 1)

            def step(t, k, f):
                if not isinstance(t, int) or t + 1 < N:
                    rows_high(t + 1, 1 - k, f)
                if not isinstance(t, int) or t < N:
                    silu_gate(t, k, f)
                if f >= 2:
                    take_y(t - 2, k, f - 2)
                if not isinstance(t, int) or t < N:
                    scale_rows(t, k, f)
                if f >= 1 and (not isinstance(t, int) or t <= N):
                    a_high(t - 1, 1 - k, f - 1)

            rows_high(0, 0, 0)
            act.wait_ge(exp_in, 1)
            sc.activation(probs[:, :, :], logits[:, :, :], ACT.Exp).then_inc(exp_out, 1)
            act.wait_ge(step_tables, 1)
            for t in range(UNROLLED):
                if t == R0:
                    act.wait_ge(step_tables, 2)
                step(t, t % 2, t)
                if t == 1:
                    high(7, 1, 6)
                if t == 4:
                    high(8, 0, 7)
            with act.Fori(0, (N - 1 - UNROLLED) // 2) as g:
                for j in range(2):
                    step(2 * g + (UNROLLED + j), (UNROLLED + j) % 2, 4)
            for t in range(N - 2, N + 2):
                step(t, t % 2, 4)

        @block.tensor
        def _(pe):
            t_ = nc.tensor
            pe.wait_ge(const_ready, 1)

            def condition(i, k, xt, f):
                pe.wait_ge(bd_ready, PB * (i + 1))
                if f:
                    pe.wait_ge(h_ready, i - 3)
                t_.matmul(pC[k][:, :], bd[:, k, :], xt, start=True, stop=True).then_inc(cond_done, 1)

            def transpose_h(i, k, s, f):
                pe.wait_ge(h_ready, i + 1)
                if f:
                    pe.wait_ge(hT_copied, i - 1)
                chunks = h[:, s, :].rearrange("p (d c) -> p c d", c=DC)
                for c in range(DC):
                    ins = t_.transpose(pH[k][:, c * P:(c + 1) * P], chunks[:, c, :], ident[:, :])
                ins.then_inc(hT_ready, 1)

            def route(i, k):
                pe.wait_ge(hT_copied, i + 1)
                o = pLogits[:, bass.ds(i * E, E)]
                for c in range(DC):
                    ins = t_.matmul(o, hT32[:, k, c * P:(c + 1) * P], router[:, c, :], start=(c == 0), stop=(c == DC - 1))
                ins.then_inc(routed, 1)

            def x_of(b, m, j):
                i = 2 * b + 2 + j
                return x_late[:, i - (NT - 4), :] if isinstance(b, int) and i >= NT - 4 else x_early[:, i, :]

            def pair(b, m, f, ahead=True, behind=True):
                if ahead:
                    for j in range(2):
                        condition(2 * b + 2 + j, (2 * m + 2 + j) % 4, x_of(b, m, j), f)
                for j in range(2):
                    transpose_h(2 * b + j, j, (2 * m + j) % 4, f)
                if behind:
                    for j in range(2):
                        route(2 * b - 2 + j, j)

            pe.wait_ge(x_loaded[0], 16)
            condition(0, 0, x_early[:, 0, :], 0)
            condition(1, 1, x_early[:, 1, :], 0)
            pair(0, 0, 0, behind=False)
            pe.wait_ge(x_loaded[1], 16)
            pe.wait_ge(router_ready, 1 + DC)
            pair(1, 1, 1)
            with pe.Fori(1, 2) as g:
                for m in range(2):
                    pair(2 * g + m, m, 1)
            pair(4, 0, 1)
            pe.wait_ge(x_loaded[2], 16)
            pair(5, 1, 1)
            pair(6, 0, 1)
            pair(7, 1, 1, ahead=False)
            route(NT - 2, 0)
            route(NT - 1, 1)

            def transpose_rows(t, k, f):
                if isinstance(t, int) and t < R0:
                    pe.wait_ge(rows_loaded[k], 16 * (t // 2 + 1))
                else:
                    pe.wait_ge(gathered[k], 8 * (t - k - R0) + 16)
                if f >= 1:
                    pe.wait_ge(rlo_ready, t - 1)
                chunks = rows[:, k, :].rearrange("p (d c) -> p c d", c=DC)
                for c in range(DC):
                    ins = t_.transpose(pH[k][:, c * P:(c + 1) * P], chunks[:, c, :], ident[:, :])
                ins.then_inc(rowsT_ready, 1)

            def step_expert(t):
                if isinstance(t, int) and (t < R0 or t >= R1):
                    return E
                if isinstance(t, int) and t == R0:
                    pe.wait_ge(step_tables, 2)
                return pe.value_load(expert[0:1, bass.ds(t, 1)], min_val=0, max_val=E)

            def gate_up(t, k, f):
                e = step_expert(t)
                pe.wait_ge(rlo_ready, t + 1)
                if f >= 2:
                    pe.wait_ge(a_ready, t - 1)
                for c in range(DC):
                    for m, (u, w) in enumerate(PARTS):
                        ins = t_.matmul(pG[k][:, :].rearrange("p (m f) -> p m f", m=2), rowsT[:, k, u, c * P:(c + 1) * P],
                                        gu_chunk(W[:, e, w, 0:GU], c),
                                        start=(c == 0 and m == 0), stop=(c == DC - 1 and m == 2))
                ins.then_inc(gu_ready, 1)

            def transpose_a(t, k, f):
                pe.wait_ge(as_ready, t + 1)
                if f >= 2:
                    pe.wait_ge(alo_ready, t - 1)
                chunks = a_scaled[:, k, :].rearrange("p (f c) -> p c f", c=FC)
                for c in range(FC):
                    ins = t_.transpose(pT[k][:, c * P:(c + 1) * P], chunks[:, c, :], ident[:, :])
                ins.then_inc(aT_ready, 1)

            def down(t, k, f):
                e = step_expert(t)
                pe.wait_ge(alo_ready, t + 1)
                if f >= 2:
                    pe.wait_ge(y_ready, t - 1)
                if isinstance(t, int) and t == 1:
                    pe.wait_ge(rank_taken, 1)
                if isinstance(t, int) and t == 2:
                    pe.wait_ge(rows_table, 1)
                for c in range(FC):
                    for m, (u, w) in enumerate(PARTS):
                        ins = t_.matmul(pY[k][:, :], aT[:, k, u, c * P:(c + 1) * P], W[:, e, w, GU + c * D:GU + (c + 1) * D],
                                        start=(c == 0 and m == 0), stop=(c == FC - 1 and m == 2))
                ins.then_inc(down_ready, 1)

            def step(t, k, f):
                if not isinstance(t, int) or t + 1 < N:
                    transpose_rows(t + 1, 1 - k, f)
                if not isinstance(t, int) or t < N:
                    gate_up(t, k, f)
                if f >= 2:
                    down(t - 2, k, f - 2)
                if f >= 1 and (not isinstance(t, int) or t <= N):
                    transpose_a(t - 1, 1 - k, f - 1)

            def ranks():
                pe.wait_ge(sel_ready, 1)
                pe.wait_ge(const_ready, 10)
                flat = sel[:, :, :].rearrange("p i e -> p (i e)")
                t_.matmul(pRank, before[:, :], flat, start=True, stop=False)
                for n in range(1, NT):
                    t_.matmul(pRank[:, n * E:], ones[:, :], flat[:, 0:(NT - n) * E], start=False, stop=(n == NT - 1))
                for n in range(NT):
                    ins = t_.matmul(pCount, ones[:, :], sel[:, n, :], start=(n == 0), stop=(n == NT - 1))
                ins.then_inc(rank_ready, 1)

            def invert():
                pe.wait_ge(one_hots_ready, 1)
                pe.wait_ge(y_ready, 1)
                for m in range(TOP * NT):
                    ins = t_.matmul(pRows, one_hot_row[:, m, :], one_hot_step[:, m, :], start=(m == 0), stop=(m == TOP * NT - 1))
                ins.then_inc(inverse_ready, 1)

            pe.wait_ge(gu_lo_ready, 1)
            pe.wait_ge(dn_lo_ready, 1)
            transpose_rows(0, 0, 0)
            for t in range(UNROLLED):
                if t == R0:
                    pe.wait_ge(gu_lo_ready, NE)
                    pe.wait_ge(dn_lo_ready, NE)
                step(t, t % 2, t)
                if t == 0:
                    ranks()
                if t == 3:
                    invert()
            with pe.Fori(0, (N - 1 - UNROLLED) // 2) as g:
                for j in range(2):
                    step(2 * g + (UNROLLED + j), (UNROLLED + j) % 2, 4)
            for t in range(N - 2, N + 2):
                step(t, t % 2, 4)


PAIR_LINKS = 19


_INS = ['x', 'itok_B_1_198', 'L0_cond_weights', 'L0_ffn_rms_weight', 'L0_ffn_router_w', 'L0_ffn_w_gate', 'L0_ffn_w_up',
        'L0_ffn_w_down', 'L0_ffn_sw_gate', 'L0_ffn_sw_up', 'L0_ffn_sw_down']


def kernel(**inputs):
    import numpy as _np
    import concourse.bacc as _bacc
    from concourse import mybir as _mybir
    from concourse.bass_utils import run_bass_kernel_spmd as _run

    nc = _bacc.Bacc("TRN2", target_bir_lowering=False, num_devices=1)
    arrays, args = {}, []
    for name in _INS:
        a = _np.ascontiguousarray(inputs[name])
        arrays[f"in_{name}_dram"] = a
        args.append(nc.dram_tensor(f"in_{name}_dram", a.shape, _mybir.dt.from_np(a.dtype), kind="ExternalInput").ap())
    shape = inputs['x'].shape
    args.append(nc.dram_tensor("out_dram", tuple(shape), _mybir.dt.float32, kind="ExternalOutput").ap())
    adaln_moe_kernel(nc, *args)
    r = _run(nc, [arrays], core_ids=[0])
    return r.results[0]["out_dram"]
```

```python
from contextlib import ExitStack

import concourse.bass as bass
from concourse import mybir
from concourse.bass import IndirectOffsetOnAxis

ALU = mybir.AluOpType
ACT = mybir.ActivationFunctionType
F32 = mybir.dt.float32
F16 = mybir.dt.float16
I32 = mybir.dt.int32
U32 = mybir.dt.uint32
AX = mybir.AxisListType

P = 128
EPS = 1e-6
H_SHIFT = 11
W_SHIFT = 14
A_SHIFT = 14
EXPONENT = 0x7F800000
RSQRT_SEED = 0x5F3759DF
TINY = 1e-30
HUGE = 1e36

PARTS = ((0, 0), (0, 1), (1, 0))


def adaln_moe_kernel(nc, x, cond, cond_w, rms_w, router_w, w_gate, w_up, w_down, s_gate, s_up, s_down, out):
    B, C, D = x.shape
    S = cond_w.shape[0]
    E, F = w_gate.shape[0], w_gate.shape[2]
    TOP = 2
    NE = E + 1
    NT = B * C // P
    PB = P // C
    ST = 3
    NP = NT // 2
    DC, FC = D // P, F // P
    GU, DN = DC * 2 * F, FC * D
    WE = GU + DN
    NR = TOP * NT + E - 1
    SA = NT // 2
    R0, R1 = SA, SA + NR
    N = NT + NR
    UNROLLED = R0 + 2
    NORM_PARTS = 12
    COMBINE_LAG = 3
    assert SA == NP and E == NP and (R1 - 1 - UNROLLED) % 2 == 0

    x_rows = x.rearrange("b c t -> (b c) t")
    out_rows = out.rearrange("b c t -> (b c) t")
    cond_rows = cond_w.rearrange("s c d -> (s c) d")
    h_rows = nc.dram_tensor("h_rows", (NT * P, D), F32).ap()
    odd_T = nc.dram_tensor("odd_T", (NP * P, 2 * D), F16).ap()
    y_routed = nc.dram_tensor("y_routed", (NR * P, D), F32).ap()
    base = nc.dram_tensor("base", (NP * P, D), F32).ap()

    with ExitStack() as ctx:
        def sb(name, shape, dt=F32):
            return ctx.enter_context(nc.sbuf_tensor(name, shape, dt))

        def psum(name):
            return ctx.enter_context(nc.psum_tensor(name, [P, D], F32))

        def sem(name):
            return ctx.enter_context(nc.semaphore(name))

        W_all = sb("W", [P, NE * 2 * WE + NP // 2 * D * 2], F16)
        W = W_all[:, 0:NE * 2 * WE].rearrange("p (e l w) -> p e l w", e=NE, l=2)
        Wf = W_all[:, :].bitcast(F32)
        x_odd = Wf[:, (NE - 2) * WE:(NE - 2) * WE + NP * D].rearrange("p (i d) -> p i d", d=D)
        x_even = Wf[:, (NE - 2) * WE + NP * D:(NE - 2) * WE + NT * D].rearrange("p (i d) -> p i d", d=D)
        y_mine = Wf[:, WE:WE + TOP * NT * D].rearrange("p (n k d) -> p n k d", n=NT, k=TOP)
        y_last = Wf[:, WE + TOP * NT * D:WE + (TOP * NT + NP) * D].rearrange("p (j d) -> p j d", d=D)
        stage = sb("stage", [P, ST, WE])
        h = sb("h", [P, 4, D])
        one_hot_row = h[:, :, :].rearrange("p s d -> p (s d)").bitcast(F16).rearrange("p (m s) -> p m s", s=P)
        sums_early = stage[:, 0:2, :].rearrange("p s w -> p (s w)").rearrange("p (j k d) -> p j k d", k=2, d=D)
        sums_late = h[:, :, :].rearrange("p (j k) d -> p j k d", k=2)
        JE = 2 * WE // (2 * D)
        oddT = sb("oddT", [P, 2, D], F16)
        rows = sb("rows", [P, 2, D])
        rowsT = sb("rowsT", [P, 2, 2, D], F16)
        a = sb("a", [P, 2, F])
        a_scaled = sb("a_scaled", [P, 2, F])
        silu = sb("silu", [P, 2, F])
        aT = sb("aT", [P, 2, 2, F], F16)
        y = sb("y", [P, 2, D])
        cw = sb("cw", [P, NT, C])
        bd = sb("bd", [P, 4, P])
        ident = sb("ident", [P, P])
        cond_i = sb("cond_i", [P, B], I32)
        cond_f = sb("cond_f", [P, B])
        row_in_c = sb("row_in_c", [P, 1])
        cond_idx = sb("cond_idx", [P, NT], U32)
        rms = sb("rms", [P, DC])
        unread = sb("unread", [P, 1])
        small_max = sb("small_max", [P, 2])
        router_raw = sb("router_raw", [P, DC, E])
        router = sb("router", [P, DC, E])
        mx = sb("mx", [P, 2, 2])
        gmx = sb("gmx", [P, 2, 2])
        mxc = sb("mxc", [P, 2])
        pw2 = sb("pw2", [P, 2])
        inv2 = sb("inv2", [P, 2])
        scl = sb("scl", [P, 2, 2])
        row_scl = sb("row_scl", [P, 2, DC])
        unscale = sb("unscale", [P, 2, NE])
        small_gmax = sb("small_gmax", [P, 2])
        router16 = sb("router16", [P, 2, DC, E], F16)
        router_pw2 = sb("router_pw2", [P, 1])
        router_scl = sb("router_scl", [P, 1])
        router_unscale = sb("router_unscale", [P, 1])
        down_scaled = sb("down_scaled", [P, DN])
        ss = sb("ss", [P, NT])
        var = sb("var", [P, 2])
        nhalf = sb("nhalf", [P, 2])
        seed = sb("seed", [P, 2], I32)
        newton = sb("newton", [P, 2])
        rstd = sb("rstd", [P, NT])
        logits = sb("logits", [P, NT, E])
        probs = sb("probs", [P, NT, E])
        pick = sb("pick", [P, NT, E])
        picks = sb("picks", [P, TOP, NT, E])
        prefer = sb("prefer", [P, NT, E])
        chosen = sb("chosen", [P, TOP, NT, E])
        red = sb("red", [P, NT])
        top = sb("top", [P, TOP, NT])
        tsum = sb("tsum", [P, NT])
        sel = sb("sel", [P, NT, E], F16)
        before = sb("before", [P, P], F16)
        ones = sb("ones", [P, P], F16)
        tiles_i = sb("tiles_i", [P, 2, E], I32)
        tiles_f = sb("tiles_f", [P, E])
        is_below = sb("is_below", [P, E, E])
        tiles_below = sb("tiles_below", [P, E, E])
        start = sb("start", [P, E])
        start_row = sb("start_row", [P, E])
        slot_e = sb("slot_e", [P, NT, E])
        slot_f = sb("slot_f", [P, TOP, NT])
        slot_i = sb("slot_i", [P, TOP, NT], I32)
        split_i = sb("split_i", [P, 2, TOP * NT], I32)
        split_f = sb("split_f", [P, 2, TOP * NT], F16)
        iota_row = sb("iota_row", [P, P], F16)
        iota_step = sb("iota_step", [P, NR], F16)
        iota_tile = sb("iota_tile", [P, NR])
        iota_e = sb("iota_e", [P, E])
        token = sb("token", [P, NT], F16)
        one_hot_step = sb("one_hot_step", [P, TOP * NT, NR], F16)
        junk = sb("junk", [P, D], F16)
        step_rows = sb("step_rows", [P, N], U32)
        expert_f = sb("expert_f", [P, NR])
        expert = sb("expert", [P, N], I32)
        is_e = sb("is_e", [P, NR, E])
        by_e = down_scaled[:, 0:2 * NR * E].rearrange("p (m t e) -> p m t e", m=2, t=NR)
        step_unscale = sb("step_unscale", [P, 2, N])
        amax = sb("amax", [P, 2])
        q = sb("q", [P, N])
        r = sb("r", [P, N])
        y_scale = sb("y_scale", [P, N])

        pG = [psum("pG0"), psum("pG1")]
        pY = [psum("pY0"), psum("pY1")]
        pH = [psum("pH0"), psum("pH1")]
        pT = [psum("pT0"), psum("pT1")]
        pC = [pG[1], pY[1], pT[0], pT[1]]
        pLogits = pH[0][:, 0:2 * E]
        pRank = pY[1][:, 0:NT * E]
        pCount = pY[1][:, NT * E:NT * E + E]
        pRows = pY[1][:, 0:NR]

        cond_loaded = sem("cond_loaded")
        small_loaded = sem("small_loaded")
        x_loaded = [sem(f"x_loaded{g}") for g in range(4)]
        pool_done = sem("pool_done")
        cond_ready = sem("cond_ready")
        idx_ready = sem("idx_ready")
        cw_loaded = [sem(f"cw_loaded{b}") for b in range(NP)]
        const_ready = sem("const_ready")
        bd_ready = sem("bd_ready")
        cond_done = sem("cond_done")
        ss_ready = sem("ss_ready")
        dve_step = sem("dve_step")
        norm_step = sem("norm_step")
        h_ready = sem("h_ready")
        h_stored = sem("h_stored")
        hT_ready = sem("hT_ready")
        odd_hi_ready = sem("odd_hi_ready")
        odd_lo_ready = sem("odd_lo_ready")
        odd_stored = sem("odd_stored")
        router_ready = sem("router_ready")
        routed = sem("routed")
        stage_loaded = [sem(f"stage_loaded{s}") for s in range(ST)]
        logits_taken = sem("logits_taken")
        small_reduced = sem("small_reduced")
        small_ready = sem("small_ready")
        wmax_ready = sem("wmax_ready")
        dmax_ready = sem("dmax_ready")
        wgmax_ready = sem("wgmax_ready")
        wscale_ready = sem("wscale_ready")
        gu_hi_ready = sem("gu_hi_ready")
        dn_hi_ready = sem("dn_hi_ready")
        gu_lo_ready = sem("gu_lo_ready")
        dn_scaled = sem("dn_scaled")
        dn_lo_ready = sem("dn_lo_ready")
        exp_in = sem("exp_in")
        exp_out = sem("exp_out")
        sel_ready = sem("sel_ready")
        rank_ready = sem("rank_ready")
        rank_taken = sem("rank_taken")
        places_ready = sem("places_ready")
        steps_marked = sem("steps_marked")
        step_hots_ready = sem("step_hots_ready")
        row_hots_ready = sem("row_hots_ready")
        inverse_ready = sem("inverse_ready")
        rows_table = sem("rows_table")
        step_tables = sem("step_tables")
        rows_loaded = [sem(f"rows_loaded{s}") for s in range(4)]
        gathered = [sem("gathered0"), sem("gathered1")]
        rowsT_ready = sem("rowsT_ready")
        rhi_ready = sem("rhi_ready")
        rlo_ready = sem("rlo_ready")
        gu_ready = sem("gu_ready")
        silu_ready = sem("silu_ready")
        a_ready = sem("a_ready")
        row_scales = sem("row_scales")
        as_ready = sem("as_ready")
        aT_ready = sem("aT_ready")
        ahi_ready = sem("ahi_ready")
        alo_ready = sem("alo_ready")
        down_ready = sem("down_ready")
        y_ready = sem("y_ready")
        y_stored = [sem("y_stored0"), sem("y_stored1")]
        sums_loaded = sem("sums_loaded")
        y_gathered = [sem(f"y_gathered{n}") for n in range(NT)]
        summed = sem("summed")
        out_written = sem("out_written")

        block = ctx.enter_context(nc.Block())

        def stored(eng, t):
            eng.wait_ge(y_stored[t % 2], 16 * (t // 2 + 1))

        def tile_of(n):
            return n + 1 - 2 * (n % 2)

        def last_T(t):
            j = t - R1
            if j % 4 < 2:
                return rows[:, j % 4, :].bitcast(F16).rearrange("p (l d) -> p l d", l=2)
            return rowsT[:, j % 2, :, :]

        def sum_of(j, k):
            return sums_early[:, j, k, :] if j < JE else sums_late[:, j - JE, k, :]

        def over_rows(ap, width):
            return ap.rearrange("p (m o) -> p m o", o=1).to_broadcast([P, ap.shape[-1], width])

        def over_choices(ap, width):
            return ap.rearrange("p (o s) -> p o s", o=1).to_broadcast([P, TOP * NT, width])

        def gu_chunk(part, c):
            return part.rearrange("p (m c f) -> p c m f", m=2, c=DC)[:, c]

        @block.sync
        def _(sp):
            sp.dma_start(cond_i[:, :], cond.rearrange("(a b) -> a b", a=1).to_broadcast([P, B])).then_inc(cond_loaded, 16)
            sp.dma_start(rms[:, :], rms_w.rearrange("(p c) -> p c", c=DC)).then_inc(small_loaded, 16)
            sp.dma_start(router_raw[:, :, :], router_w.rearrange("(p c) e -> p c e", c=DC)).then_inc(small_loaded, 16)

            x_pairs = x_rows.rearrange("(j k p) t -> p j k t", k=2, p=P)
            out_pairs = out_rows.rearrange("(j k p) t -> p j k t", k=2, p=P)
            base_tiles = base.rearrange("(j p) t -> p j t", p=P)

            def load_x(g, lo, hi):
                sp.dma_start(x_even[:, lo:hi, :], x_pairs[:, lo:hi, 0, :]).then_inc(x_loaded[g], 16)
                sp.dma_start(x_odd[:, lo:hi, :], x_pairs[:, lo:hi, 1, :]).then_inc(x_loaded[g], 16)

            def load_expert(n, gate, up, down):
                s = n % ST
                sp.dma_start(stage[:, s, 0:DC * F], gate.rearrange("(p c) f -> p (c f)", c=DC)).then_inc(stage_loaded[s], 16)
                sp.dma_start(stage[:, s, DC * F:GU], up.rearrange("(p c) f -> p (c f)", c=DC)).then_inc(stage_loaded[s], 16)
                sp.dma_start(stage[:, s, GU:WE], down.rearrange("(p c) d -> p (c d)", c=FC)).then_inc(stage_loaded[s], 16)

            load_x(0, 0, 1)
            sp.wait_ge(cw_loaded[0], 32)
            load_expert(0, s_gate, s_up, s_down)
            load_x(3, 1, 2)
            load_expert(1, w_gate[0], w_up[0], w_down[0])
            load_x(1, 2, 4)
            load_expert(2, w_gate[1], w_up[1], w_down[1])

            def store_h(b, m):
                s = 2 * m
                sp.wait_ge(h_ready, 2 * b + 2)
                if b:
                    sp.wait_ge(h_stored, 16 * b)
                sp.dma_start(h_rows[b * 2 * P:(b + 1) * 2 * P, :].rearrange("(i p) t -> p i t", p=P),
                             h[:, s:s + 2, :]).then_inc(h_stored, 16)

            def next_weights(b):
                sp.wait_ge(gu_lo_ready, b + 1)
                sp.wait_ge(dn_lo_ready, b + 1)
                e = b + ST - 1
                load_expert(b + ST, w_gate[e], w_up[e], w_down[e])

            def store_y(t, k):
                sp.wait_ge(y_ready, t + 1)
                dst = base[t * P:(t + 1) * P, :] if isinstance(t, int) and t < R0 else y_routed[bass.ds((t - R0) * P, P), :]
                sp.dma_start(dst, y[:, k, :]).then_inc(y_stored[k], 16)

            for b in range(NP):
                store_h(b, b % 2)
                if b >= 3:
                    store_y(b - 3, (b - 3) % 2)
                sp.wait_ge(odd_lo_ready, b + 1)
                sp.dma_start(odd_T[b * P:(b + 1) * P, :], oddT[:, :, :].rearrange("p l d -> p (l d)")).then_inc(odd_stored, 16)
                if b == 0:
                    load_x(2, 4, NP)
                if b + ST < NE:
                    next_weights(b)
            for t in range(NP - 3, NP):
                store_y(t, t % 2)

            def load_rows(t):
                j = t - R1
                if j < 2:
                    sp.wait_ge(rowsT_ready, NR)
                else:
                    sp.wait_ge(gu_ready, R1 + max(0, j - 3))
                sp.dma_start(last_T(t), odd_T[j * P:(j + 1) * P, :].rearrange("p (l d) -> p l d", l=2)).then_inc(rows_loaded[j % 4], 16)

            sp.wait_ge(gu_lo_ready, NE)
            sp.wait_ge(dn_lo_ready, NE)
            sp.wait_ge(inverse_ready, 1)
            stored(sp, NP - 2)
            stored(sp, NP - 1)
            with sp.Fori(0, JE) as j:
                store_y(2 * j + R0, 0)
                sp.dma_start(sums_early[:, bass.ds(j, 1), 0, :], x_pairs[:, bass.ds(j, 1), 1, :]).then_inc(sums_loaded, 16)
                store_y(2 * j + (R0 + 1), 1)
                sp.dma_start(sums_early[:, bass.ds(j, 1), 1, :], base_tiles[:, bass.ds(j, 1), :]).then_inc(sums_loaded, 16)
            for j in range(JE, NP):
                store_y(2 * j + R0, 0)
                sp.dma_start(sums_late[:, j - JE, 0, :], x_pairs[:, j, 1, :]).then_inc(sums_loaded, 16)
                store_y(2 * j + R0 + 1, 1)
                sp.dma_start(sums_late[:, j - JE, 1, :], base_tiles[:, j, :]).then_inc(sums_loaded, 16)

            with sp.Fori(R0 // 2 + NP, (R1 - 5) // 2) as g:
                for k in range(2):
                    store_y(2 * g + k, k)
            sp.wait_ge(odd_stored, 16 * NP)
            store_y(R1 - 5, (R1 - 5) % 2)
            load_rows(R1)
            load_rows(R1 + 1)
            store_y(R1 - 4, (R1 - 4) % 2)
            store_y(R1 - 3, (R1 - 3) % 2)
            load_rows(R1 + 2)
            load_rows(R1 + 3)
            store_y(R1 - 2, (R1 - 2) % 2)
            store_y(R1 - 1, (R1 - 1) % 2)
            for t in range(R1 + 4, N):
                load_rows(t)

            for j in range(NP):
                for k in (1, 0):
                    sp.wait_ge(summed, 5 * j + 5 - k)
                    sp.dma_start(out_pairs[:, j, 1 - k, :], sum_of(j, k)).then_inc(out_written, 16)
            sp.wait_ge(out_written, 16 * NT)

        @block.gpsimd
        def _(pool):
            g_ = nc.gpsimd
            small = dict(allow_small_or_imprecise_dtypes=True)
            g_.memset(ident[:, :], 0.0).then_inc(pool_done, 1)
            g_.memset(before[:, :], 1.0).then_inc(pool_done, 1)
            g_.memset(bd[:, :, :], 0.0).then_inc(pool_done, 1)
            for b in range(PB):
                pool.wait_ge(pool_done, 3 + b)
                g_.iota(row_in_c[b * C:(b + 1) * C, :], [[0, 1]], base=0, channel_multiplier=1, **small).then_inc(pool_done, 1)
            pool.wait_ge(pool_done, 3 + PB)
            pool.wait_ge(cond_ready, 1)
            for b in range(PB):
                if b:
                    pool.wait_ge(idx_ready, b)
                part = slice(b * C, (b + 1) * C)
                mine = cond_f[part, :].rearrange("p (i b) -> p b i", b=PB)[:, b, :]
                g_.tensor_scalar(cond_idx[part, :], mine, float(C), row_in_c[part, 0:1],
                                 ALU.mult, ALU.add).then_inc(idx_ready, 1)
            pool.wait_ge(idx_ready, PB)

            def gather_cond(g):
                for i in range(2 * g, 2 * g + 2):
                    g_.indirect_dma_start(out=cw[:, i, :], out_offset=None, in_=cond_rows,
                                          in_offset=IndirectOffsetOnAxis(ap=cond_idx[:, i:i + 1], axis=0)
                                          ).then_inc(cw_loaded[g], 16)

            gather_cond(0)
            gather_cond(1)
            g_.affine_select(out=ident[:, :], in_=ident[:, :], compare_op=ALU.not_equal, fill=1.0,
                             base=0, pattern=[[-1, P]], channel_multiplier=1).then_inc(const_ready, 1)
            gather_cond(2)
            gather_cond(3)

            def reduce_max(n, k):
                pool.wait_ge(wmax_ready, n + 1)
                pool.wait_ge(dmax_ready, n + 1)
                g_.partition_all_reduce(gmx[:, k, :], mx[:, k, :], P, bass.bass_isa.ReduceOp.max).then_inc(wgmax_ready, 1)

            def down_low(n, k):
                pool.wait_ge(wscale_ready, n + 1)
                g_.tensor_scalar(down_scaled[:, :], stage[:, n % ST, GU:WE], scl[:, k, 1:2], None, ALU.mult).then_inc(dn_scaled, 1)
                pool.wait_ge(dn_hi_ready, n + 1)
                pool.wait_ge(dn_scaled, n + 1)
                g_.tensor_tensor(W[:, n, 1, GU:WE], down_scaled[:, :], W[:, n, 0, GU:WE], ALU.subtract).then_inc(dn_lo_ready, 1)

            pool.wait_ge(small_reduced, 1)
            g_.partition_all_reduce(small_gmax[:, :], small_max[:, :], P, bass.bass_isa.ReduceOp.max).then_inc(small_ready, 1)
            reduce_max(0, 0)
            g_.affine_select(out=before[:, :], in_=before[:, :], compare_op=ALU.is_gt, fill=0.0,
                             base=0, pattern=[[1, P]], channel_multiplier=-1).then_inc(const_ready, 1)
            g_.memset(ones[:, :], 1.0).then_inc(const_ready, 1)
            g_.iota(iota_row[:, :], [[1, P]], base=0, channel_multiplier=0, **small).then_inc(const_ready, 1)
            g_.iota(iota_step[:, :], [[1, NR]], base=0, channel_multiplier=0, **small).then_inc(const_ready, 1)
            g_.iota(iota_tile[:, :], [[1, NR]], base=0, channel_multiplier=0, **small).then_inc(const_ready, 1)
            g_.iota(iota_e[:, :], [[1, E]], base=0, channel_multiplier=0, **small).then_inc(const_ready, 1)
            g_.iota(token[:, :], [[P, NT]], base=0, channel_multiplier=1, **small).then_inc(const_ready, 1)
            g_.memset(expert[:, :], 0).then_inc(const_ready, 1)
            for n in range(NE):
                down_low(n, n % 2)
                if n + 1 < NE:
                    reduce_max(n + 1, (n + 1) % 2)
                if n < 2:
                    gather_cond(4 + 2 * n)
                    gather_cond(5 + 2 * n)

            pool.wait_ge(steps_marked, 1)
            for k in range(TOP):
                mine = one_hot_step[:, k * NT:(k + 1) * NT, :]
                g_.tensor_tensor(mine, mine, over_rows(token[:, :], NR), ALU.mult).then_inc(step_hots_ready, 1)

            pool.wait_ge(rows_table, 1)
            pool.wait_ge(h_stored, 16 * NP)
            for t in range(R0, R1):
                if t >= R0 + 2:
                    pool.wait_ge(rowsT_ready, t - R0 - 1)
                g_.indirect_dma_start(out=rows[:, t % 2, :], out_offset=None, in_=h_rows,
                                      in_offset=IndirectOffsetOnAxis(ap=step_rows[:, t:t + 1], axis=0)
                                      ).then_inc(gathered[t % 2], 16)

            pool.wait_ge(down_ready, R1)
            for t in (R1 - 2, R1 - 1):
                stored(pool, t)
            for n in range(NT):
                i = tile_of(n)
                for k in range(TOP):
                    g_.indirect_dma_start(out=y_mine[:, n, k, :], out_offset=None, in_=y_routed,
                                          in_offset=IndirectOffsetOnAxis(ap=slot_i[:, k, i:i + 1].bitcast(U32), axis=0)
                                          ).then_inc(y_gathered[n], 16)

        @block.vector
        def _(dve):
            v = nc.vector
            links = [0]

            def link(ins):
                links[0] += 1
                ins.then_inc(dve_step, 1)
                dve.wait_ge(dve_step, links[0])

            dve.wait_ge(cond_loaded, 16)
            link(v.tensor_scalar(cond_f[:, :], cond_i[:, :], 0.0, float(S), ALU.is_lt, ALU.mult))
            link(v.tensor_tensor(cond_f[:, :], cond_f[:, :], cond_i[:, :], ALU.add))
            v.tensor_scalar(cond_f[:, :], cond_f[:, :], 0.0, S - 1.0, ALU.max, ALU.min).then_inc(cond_ready, 1)

            dve.wait_ge(small_loaded, 32)
            v.tensor_reduce(small_max[:, 0:1], rms[:, :], AX.X, ALU.max, apply_absolute_value=True)
            for c in range(DC):
                ins = v.tensor_scalar(router[:, c, :], router_raw[:, c, :], rms[:, c:c + 1], None, ALU.mult)
            link(ins)
            v.tensor_reduce(small_max[:, 1:2], router[:, :, :].rearrange("p c e -> p (c e)"), AX.X, ALU.max,
                            apply_absolute_value=True).then_inc(small_reduced, 1)

            def split_router():
                dve.wait_ge(small_ready, 1)
                link(v.tensor_scalar(router_pw2[:, :], small_gmax[:, 1:2], TINY, HUGE, ALU.max, ALU.min))
                link(v.tensor_scalar(router_pw2[:, :].bitcast(U32), router_pw2[:, :].bitcast(U32), EXPONENT, None, ALU.bitwise_and))
                v.tensor_scalar(router_unscale[:, :], router_pw2[:, :], float(2.0 ** -(W_SHIFT + H_SHIFT)), None, ALU.mult)
                link(v.reciprocal(router_scl[:, :], router_pw2[:, :]))
                link(v.tensor_scalar(router_scl[:, :], router_scl[:, :], float(2 ** W_SHIFT), None, ALU.mult))
                link(v.tensor_scalar(router16[:, 0], router[:, :, :], router_scl[:, 0:1], None, ALU.mult))
                v.scalar_tensor_tensor(router16[:, 1], router[:, :, :], router_scl[:, 0:1], router16[:, 0],
                                       ALU.mult, ALU.subtract).then_inc(router_ready, 1)

            def weight_scale(n, k):
                dve.wait_ge(wgmax_ready, n + 1)
                v.tensor_scalar(mxc[:, 1:2], gmx[:, k, 1:2], TINY, HUGE, ALU.max, ALU.min)
                link(v.tensor_scalar(mxc[:, 0:1], gmx[:, k, 0:1], small_gmax[:, 0:1], TINY, ALU.mult, ALU.max))
                link(v.tensor_scalar(mxc[:, 0:1], mxc[:, 0:1], HUGE, None, ALU.min))
                link(v.tensor_scalar(pw2[:, :].bitcast(U32), mxc[:, :].bitcast(U32), EXPONENT, None, ALU.bitwise_and))
                v.tensor_scalar(unscale[:, 0, n:n + 1], pw2[:, 0:1], float(2.0 ** -(W_SHIFT + H_SHIFT)), None, ALU.mult)
                v.tensor_scalar(unscale[:, 1, n:n + 1], pw2[:, 1:2], float(2.0 ** -W_SHIFT), None, ALU.mult)
                link(v.reciprocal(inv2[:, :], pw2[:, :]))
                link(v.tensor_scalar(scl[:, k, :], inv2[:, :], float(2 ** W_SHIFT), None, ALU.mult))
                v.tensor_scalar(row_scl[:, k, :], rms[:, :], scl[:, k, 0:1], None, ALU.mult).then_inc(wscale_ready, 1)

            def down_max(n, k):
                dve.wait_ge(stage_loaded[n % ST], 48 * (n // ST + 1))
                if n >= 2:
                    dve.wait_ge(wgmax_ready, n - 1)
                v.tensor_reduce(mx[:, k, 1:2], stage[:, n % ST, GU:WE], AX.X, ALU.max, apply_absolute_value=True).then_inc(dmax_ready, 1)

            def gate_up_low(n, k, between=lambda c: None):
                dve.wait_ge(wscale_ready, n + 1)
                for c in range(DC):
                    between(c)
                    dve.wait_ge(gu_hi_ready, DC * n + c + 1)
                    ins = v.scalar_tensor_tensor(gu_chunk(W[:, n, 1, 0:GU], c), gu_chunk(stage[:, n % ST, 0:GU], c),
                                                 row_scl[:, k, c:c + 1], gu_chunk(W[:, n, 0, 0:GU], c),
                                                 ALU.mult, ALU.subtract)
                ins.then_inc(gu_lo_ready, 1)

            def norm_factors(b, parts=range(NORM_PARTS)):
                k = float(2.0 ** (-2 * H_SHIFT))
                f = rstd[:, 2 * b:2 * b + 2]
                for i in parts:
                    if i == 0:
                        dve.wait_ge(ss_ready, 2 * b + 2)
                        ins = v.tensor_scalar(var[:, :], ss[:, 2 * b:2 * b + 2], k / D, k * EPS, ALU.mult, ALU.add)
                    else:
                        dve.wait_ge(norm_step, NORM_PARTS * b + i)
                    if i == 1:
                        v.tensor_scalar(nhalf[:, :], var[:, :], -0.5, None, ALU.mult)
                        ins = v.tensor_scalar(seed[:, :], var[:, :].bitcast(I32), 1, None, ALU.logical_shift_right)
                    if i == 2:
                        ins = v.tensor_scalar(f.bitcast(I32), seed[:, :], -1.0, float(RSQRT_SEED), ALU.mult, ALU.add)
                    if i >= 3 and i % 3 == 0:
                        ins = v.tensor_tensor(newton[:, :], f, f, ALU.mult)
                    if i >= 3 and i % 3 == 1:
                        ins = v.tensor_tensor(newton[:, :], newton[:, :], nhalf[:, :], ALU.mult)
                    if i >= 3 and i % 3 == 2:
                        ins = v.scalar_tensor_tensor(f, newton[:, :], 1.5, f, ALU.add, ALU.mult)
                    ins.then_inc(norm_step, 1)

            def odd_low(b):
                dve.wait_ge(odd_hi_ready, b + 1)
                v.tensor_tensor(oddT[:, 1, :], pH[1][:, :], oddT[:, 0, :], ALU.subtract).then_inc(odd_lo_ready, 1)

            def diagonal(i, k):
                for b in range(PB):
                    part = slice(b * C, (b + 1) * C)
                    v.tensor_copy(bd[part, k, b * C:(b + 1) * C], cw[part, i, :]).then_inc(bd_ready, 1)

            def diagonals(b, m):
                for j in range(2):
                    dve.wait_ge(cond_done, 2 * b + j + 1)
                    diagonal(2 * b + 4 + j, 2 * m + j)

            def rows_low(t, k, bank):
                dve.wait_ge(rhi_ready, t + 1)
                v.tensor_tensor(rowsT[:, k, 1, :], pH[bank][:, :], rowsT[:, k, 0, :], ALU.subtract).then_inc(rlo_ready, 1)

            def gated(t, k, f, bank):
                dve.wait_ge(silu_ready, t + 1)
                if f >= 2:
                    dve.wait_ge(as_ready, t - 1)
                one = bass.ds(t, 1)
                v.scalar_tensor_tensor(a[:, k, :], pG[bank][:, F:2 * F], step_unscale[:, 0, one], silu[:, k, :],
                                       ALU.mult, ALU.mult).then_inc(a_ready, 1)
                dve.wait_ge(a_ready, t + 1)
                v.tensor_reduce(amax[:, k:k + 1], a[:, k, :], AX.X, ALU.max, apply_absolute_value=True).then_inc(row_scales, 1)
                dve.wait_ge(row_scales, 4 * t + 1)
                v.tensor_scalar(q[:, one], amax[:, k:k + 1], TINY, float(2.0 ** -A_SHIFT), ALU.max, ALU.mult).then_inc(row_scales, 1)
                dve.wait_ge(row_scales, 4 * t + 2)
                v.reciprocal(r[:, one], q[:, one]).then_inc(row_scales, 1)
                v.tensor_tensor(y_scale[:, one], q[:, one], step_unscale[:, 1, one], ALU.mult).then_inc(row_scales, 1)

            def a_low(t, k, source):
                dve.wait_ge(ahi_ready, t + 1)
                v.tensor_tensor(aT[:, k, 1, :], source[:, 0:F], aT[:, k, 0, :], ALU.subtract).then_inc(alo_ready, 1)

            def take_base(t, k, f):
                dve.wait_ge(down_ready, t + 1)
                dve.wait_ge(row_scales, 4 * t + 4)
                if f >= 2:
                    dve.wait_ge(y_stored[k], 16 * (t // 2))
                v.scalar_tensor_tensor(y[:, k, :], pY[0][:, :], y_scale[:, t:t + 1], x_even[:, t, :],
                                       ALU.mult, ALU.add).then_inc(y_ready, 1)

            def take_logits(b):
                dve.wait_ge(routed, b + 1)
                v.tensor_scalar(logits[:, 2 * b:2 * b + 2, :], pLogits.rearrange("p (i e) -> p i e", e=E),
                                router_unscale[:, 0:1], None, ALU.mult).then_inc(logits_taken, 1)

            def pair(b, m):
                def norm(*parts):
                    if b + 1 < NP:
                        norm_factors(b + 1, parts)

                if b + 2 < NP:
                    dve.wait_ge(cw_loaded[b + 2], 32)
                    diagonals(b, m)
                if b >= 3:
                    take_base(b - 3, 1 - m, b - 3)
                down_max(b + 1, 1 - m)
                norm(0, 1, 2, 3, 4)
                gate_up_low(b, m, lambda c: norm(5 + c))
                norm(9)
                rows_low(b, m, 0)
                norm(10)
                odd_low(b)
                norm(11)
                if b >= 2:
                    a_low(b - 2, m, pY[0])
                if b >= 1:
                    gated(b - 1, 1 - m, b - 1, 0)
                take_logits(b)
                weight_scale(b + 1, 1 - m)

            def step(t, k):
                inside = isinstance(t, int)
                if not inside or t + 1 < R1:
                    rows_low(t + 1, 1 - k, 1 - k)
                if not inside or t < N:
                    gated(t, k, 2, k)
                if not inside or (t > R0 and t <= N):
                    a_low(t - 1, 1 - k, pT[1 - k])

            def wide(ap):
                return ap.rearrange("p (i o) -> p i o", o=1).to_broadcast([P, NT, E])

            def exp_input():
                dve.wait_ge(logits_taken, NP)
                link(v.tensor_reduce(red[:, :], logits[:, :, :], AX.X, ALU.max))
                v.tensor_tensor(logits[:, :, :], logits[:, :, :], wide(red[:, :]), ALU.subtract).then_inc(exp_in, 1)
                for e in range(E):
                    ins = v.memset(prefer[:, :, e], float(E - e))
                dve.wait_ge(const_ready, 9)
                link(ins)

            def choose():
                dve.wait_ge(exp_out, 1)
                link(v.tensor_reduce(red[:, :], probs[:, :, :], AX.X, ALU.add))
                link(v.reciprocal(red[:, :], red[:, :]))
                link(v.tensor_tensor(probs[:, :, :], probs[:, :, :], wide(red[:, :]), ALU.mult))
                for k in range(TOP):
                    link(v.tensor_reduce(top[:, k, :], probs[:, :, :], AX.X, ALU.max))
                    link(v.tensor_tensor(pick[:, :, :], probs[:, :, :], wide(top[:, k, :]), ALU.is_equal))
                    link(v.tensor_tensor(pick[:, :, :], pick[:, :, :], prefer[:, :, :], ALU.mult))
                    link(v.tensor_reduce(red[:, :], pick[:, :, :], AX.X, ALU.max))
                    link(v.tensor_tensor(chosen[:, k], prefer[:, :, :], wide(red[:, :]), ALU.is_equal))
                    if k == 0:
                        link(v.scalar_tensor_tensor(probs[:, :, :], chosen[:, k], -2.0, probs[:, :, :], ALU.mult, ALU.add))
                v.tensor_tensor(sel[:, :, :], chosen[:, 0], chosen[:, 1], ALU.add).then_inc(sel_ready, 1)
                link(v.tensor_tensor(tsum[:, :], top[:, 0, :], top[:, 1, :], ALU.add))
                link(v.reciprocal(tsum[:, :], tsum[:, :]))
                for k in range(TOP):
                    link(v.tensor_tensor(top[:, k, :], top[:, k, :], tsum[:, :], ALU.mult))

            def place():
                dve.wait_ge(rank_ready, 1)
                link(v.tensor_scalar(tiles_i[:, 0, :], pCount, float(P - 1), None, ALU.add))
                link(v.tensor_scalar(tiles_i[:, 1, :], tiles_i[:, 0, :], P.bit_length() - 1, None, ALU.logical_shift_right))
                link(v.tensor_copy(tiles_f[:, :], tiles_i[:, 1, :]))
                link(v.tensor_tensor(tiles_below[:, :, :], is_below[:, :, :],
                                     tiles_f[:, :].rearrange("p (o e) -> p o e", o=1).to_broadcast([P, E, E]), ALU.mult))
                link(v.tensor_reduce(start[:, :], tiles_below[:, :, :], AX.X, ALU.add))
                link(v.tensor_scalar(start_row[:, :], start[:, :], float(P), None, ALU.mult))
                by_tile = start_row[:, :].rearrange("p (o e) -> p o e", o=1).to_broadcast([P, NT, E])
                v.tensor_tensor(slot_e[:, :, :], pRank.rearrange("p (i e) -> p i e", e=E), by_tile, ALU.add).then_inc(rank_taken, 1)
                dve.wait_ge(rank_taken, 1)
                each = slot_e[:, :, :].rearrange("p (o i) e -> p o (i e)", o=1).to_broadcast([P, TOP, NT * E])
                flat_picks = picks[:, :, :, :].rearrange("p k i e -> p k (i e)")
                link(v.tensor_tensor(flat_picks, chosen[:, :, :, :].rearrange("p k i e -> p k (i e)"), each, ALU.mult))
                link(v.tensor_reduce(slot_f[:, :, :].rearrange("p k i -> p (k i)"),
                                     picks[:, :, :, :].rearrange("p k i e -> p (k i) e"), AX.X, ALU.add))
                link(v.tensor_copy(slot_i[:, :, :], slot_f[:, :, :]))
                flat = slot_i[:, :, :].rearrange("p k i -> p (k i)")
                v.tensor_scalar(split_i[:, 0, :], flat, P - 1, None, ALU.bitwise_and)
                link(v.tensor_scalar(split_i[:, 1, :], flat, P.bit_length() - 1, None, ALU.logical_shift_right))
                v.tensor_copy(split_f[:, :, :], split_i[:, :, :]).then_inc(places_ready, 1)
                dve.wait_ge(places_ready, 1)
                dve.wait_ge(h_stored, 16 * NP)
                v.tensor_tensor(one_hot_step[:, :, :], over_choices(iota_step[:, :], NR), over_rows(split_f[:, 1, :], NR),
                                ALU.is_equal).then_inc(steps_marked, 1)
                v.tensor_tensor(one_hot_row[:, :, :], over_choices(iota_row[:, :], P), over_rows(split_f[:, 0, :], P),
                                ALU.is_equal).then_inc(row_hots_ready, 1)

            def routed_rows():
                dve.wait_ge(inverse_ready, 1)
                v.tensor_copy(step_rows[:, R0:R1], pRows).then_inc(rows_table, 1)

            def tables():
                steps_over = iota_tile[:, :].rearrange("p (t o) -> p t o", o=1)
                started = is_e[:, :, 0:E - 1]
                link(v.tensor_tensor(started, steps_over.to_broadcast([P, NR, E - 1]),
                                     start[:, 1:E].rearrange("p (o e) -> p o e", o=1).to_broadcast([P, NR, E - 1]), ALU.is_ge))
                link(v.tensor_reduce(expert_f[:, :], started, AX.X, ALU.add))
                v.tensor_scalar(expert[:, R0:R1], expert_f[:, :], 1.0, None, ALU.add)
                link(v.tensor_tensor(is_e[:, :, :], expert_f[:, :].rearrange("p (t o) -> p t o", o=1).to_broadcast([P, NR, E]),
                                     iota_e[:, :].rearrange("p (o e) -> p o e", o=1).to_broadcast([P, NR, E]), ALU.is_equal))
                dve.wait_ge(dn_lo_ready, NE)
                for m in range(2):
                    ins = v.tensor_tensor(by_e[:, m], is_e[:, :, :],
                                          unscale[:, m, 1:NE].rearrange("p (o e) -> p o e", o=1).to_broadcast([P, NR, E]), ALU.mult)
                link(ins)
                v.tensor_reduce(step_unscale[:, :, R0:R1], by_e[:, :, :, :], AX.X, ALU.add).then_inc(step_tables, 1)

            def shared_unscale():
                for m in range(2):
                    for lo, hi in ((0, R0), (R1, N)):
                        ins = v.tensor_scalar(step_unscale[:, m, lo:hi], amax[:, 0:1].to_broadcast([P, hi - lo]), 0.0,
                                              unscale[:, m, 0:1], ALU.mult, ALU.add)
                link(ins)
                v.memset(amax[:, :], 0.0).then_inc(step_tables, 1)

            def combine(j, part):
                k, what = ((0, -1), (1, 0), (0, 0), (1, 1), (0, 1))[part]
                o = sum_of(j, k)
                if j == 0 and part == 0:
                    dve.wait_ge(sums_loaded, 16 * NT)
                if part >= 2:
                    dve.wait_ge(summed, 5 * j + part - 1)
                if what < 0:
                    dve.wait_ge(y_ready, R1 + j + 1)
                    v.tensor_tensor(o, o, y_last[:, j, :], ALU.add).then_inc(summed, 1)
                    return
                n = 2 * j + k
                dve.wait_ge(y_gathered[n], 32)
                i = tile_of(n)
                v.scalar_tensor_tensor(o, y_mine[:, n, what, :], top[:, what, i:i + 1], o, ALU.mult, ALU.add).then_inc(summed, 1)

            dve.wait_ge(pool_done, 3 + PB)
            link(v.memset(amax[:, :], 0.0))
            for i in range(4):
                if i % 2 == 0:
                    dve.wait_ge(cw_loaded[i // 2], 32)
                diagonal(i, i)
            norm_factors(0)
            down_max(0, 0)
            split_router()
            weight_scale(0, 0)
            dve.wait_ge(const_ready, 9)
            link(v.tensor_tensor(is_below[:, :, :], iota_e[:, :].rearrange("p (e o) -> p e o", o=1).to_broadcast([P, E, E]),
                                 iota_e[:, :].rearrange("p (o e) -> p o e", o=1).to_broadcast([P, E, E]), ALU.is_gt))
            shared_unscale()
            for b in range(NP):
                pair(b, b % 2)

            exp_input()
            take_base(R0 - 3, 1, 2)
            choose()
            a_low(R0 - 2, 0, pY[0])
            place()
            gated(R0 - 1, 1, 2, 0)
            take_base(R0 - 2, 0, 2)
            routed_rows()
            gate_up_low(NE - 1, 0)
            a_low(R0 - 1, 1, pY[0])
            tables()
            take_base(R0 - 1, 1, 2)

            rows_low(R0, 0, 0)
            step(R0, 0)
            step(R0 + 1, 1)
            with dve.Fori(0, (R1 - 1 - UNROLLED) // 2) as g:
                for j in range(2):
                    step(2 * g + (UNROLLED + j), j)
            for t in range(R1 - 1, N + 1):
                j = t - R1 - COMBINE_LAG
                if t < N:
                    gated(t, t % 2, 2, t % 2)
                if j >= 0:
                    combine(j, 0)
                a_low(t - 1, (t - 1) % 2, pT[(t - 1) % 2])
                if j >= 0:
                    for part in range(1, 5):
                        combine(j, part)
            for j in range(N + 1 - R1 - COMBINE_LAG, NP):
                for part in range(5):
                    combine(j, part)

        @block.scalar
        def _(act):
            sc = nc.scalar

            def square(i, k):
                act.wait_ge(cond_done, i + 1)
                if i > 0:
                    act.wait_ge(ss_ready, i)
                sc.activation(junk[:, :], pC[k][:, :], ACT.Square, accum_out=ss[:, i:i + 1]).then_inc(ss_ready, 1)

            def normalise(b, j, m, f):
                i, k = 2 * b + j, 2 * m + j
                act.wait_ge(norm_step, NORM_PARTS * (b + 1))
                if f >= 2:
                    act.wait_ge(hT_ready, i - 3)
                    act.wait_ge(h_stored, 16 * (b - 1))
                sc.activation(h[:, k, :], pC[k][:, :], ACT.Copy, scale=rstd[:, i:i + 1]).then_inc(h_ready, 1)

            def weight_sums(n, k):
                act.wait_ge(stage_loaded[n % ST], 48 * (n // ST + 1))
                sc.activation(W[:, n, 0, 0:GU], stage[:, n % ST, 0:GU], ACT.Abs, accum_out=mx[:, k, 0:1]).then_inc(wmax_ready, 1)

            def high(n, k):
                act.wait_ge(wscale_ready, n + 1)
                for c in range(DC):
                    sc.activation(gu_chunk(W[:, n, 0, 0:GU], c), gu_chunk(stage[:, n % ST, 0:GU], c), ACT.Copy,
                                  scale=row_scl[:, k, c:c + 1]).then_inc(gu_hi_ready, 1)
                sc.activation(W[:, n, 0, GU:WE], stage[:, n % ST, GU:WE], ACT.Copy, scale=scl[:, k, 1:2]).then_inc(dn_hi_ready, 1)

            def rows_high(t, k, f, bank):
                if f >= 2:
                    act.wait_ge(gu_ready, t - 1)
                sc.activation(rowsT[:, k, 0, :], pH[bank][:, :], ACT.Copy).then_inc(rhi_ready, 1)

            def odd_high(b):
                act.wait_ge(hT_ready, 2 * b + 2)
                if b >= 1:
                    act.wait_ge(routed, b)
                    act.wait_ge(odd_stored, 16 * b)
                sc.activation(oddT[:, 0, :], pH[1][:, :], ACT.Copy).then_inc(odd_hi_ready, 1)

            def silu_gate(t, k, f, bank):
                act.wait_ge(gu_ready, t + 1)
                if f >= 2:
                    act.wait_ge(a_ready, t - 1)
                sc.activation(silu[:, k, :], pG[bank][:, 0:F], ACT.Silu, scale=step_unscale[:, 0, bass.ds(t, 1)]).then_inc(silu_ready, 1)

            def scale_rows(t, k, f):
                act.wait_ge(row_scales, 4 * t + 3)
                if f >= 2:
                    act.wait_ge(aT_ready, t - 1)
                sc.activation(a_scaled[:, k, :], a[:, k, :], ACT.Copy, scale=r[:, bass.ds(t, 1)]).then_inc(as_ready, 1)

            def a_high(t, k, f, source):
                act.wait_ge(aT_ready, t + 1)
                if f >= 2:
                    act.wait_ge(down_ready, t - 1)
                sc.activation(aT[:, k, 0, :], source[:, 0:F], ACT.Copy).then_inc(ahi_ready, 1)

            def take_y(t, k):
                act.wait_ge(down_ready, t + 1)
                act.wait_ge(row_scales, 4 * t + 4)
                last = isinstance(t, int) and t >= R1
                if not last:
                    act.wait_ge(y_stored[k], 16 * (t // 2) if isinstance(t, int) else 8 * (t - k))
                dst = y_last[:, t - R1, :] if last else y[:, k, :]
                sc.activation(dst, pY[k][:, :], ACT.Copy, scale=y_scale[:, bass.ds(t, 1)]).then_inc(y_ready, 1)

            def pair(b, m):
                for j in range(2):
                    normalise(b, j, m, b)
                if b >= 2:
                    scale_rows(b - 2, m, b - 2)
                if b + 1 < NP:
                    for j in range(2):
                        square(2 * b + 2 + j, 2 * (1 - m) + j)
                high(b, m)
                act.wait_ge(hT_ready, 2 * b + 1)
                rows_high(b, m, b, 0)
                odd_high(b)
                if b >= 2:
                    a_high(b - 2, m, b - 2, pY[0])
                if b >= 1:
                    silu_gate(b - 1, 1 - m, b - 1, 0)
                if b == NP - 1:
                    act.wait_ge(y_ready, NP // 2)
                weight_sums(b + 1, 1 - m)

            act.wait_ge(small_loaded, 32)
            sc.activation(unread[:, :], rms[:, 0:1], ACT.Silu)
            square(0, 0)
            square(1, 1)
            weight_sums(0, 0)
            for b in range(NP):
                pair(b, b % 2)

            scale_rows(R0 - 2, 0, 2)
            act.wait_ge(exp_in, 1)
            sc.activation(probs[:, :, :], logits[:, :, :], ACT.Exp).then_inc(exp_out, 1)
            a_high(R0 - 2, 0, 2, pY[0])
            high(NE - 1, 0)
            silu_gate(R0 - 1, 1, 2, 0)
            scale_rows(R0 - 1, 1, 2)
            a_high(R0 - 1, 1, 2, pY[0])

            def step(t, k):
                inside = isinstance(t, int)
                if not inside or t + 1 < R1:
                    act.wait_ge(rowsT_ready, t + 2 - R0)
                    rows_high(t + 1, 1 - k, 2, 1 - k)
                if not inside or t < N:
                    silu_gate(t, k, 2, k)
                if not inside or t >= R0 + 2:
                    take_y(t - 2, k)
                if not inside or t < N:
                    scale_rows(t, k, 2)
                if not inside or (t > R0 and t <= N):
                    a_high(t - 1, 1 - k, 2, pT[1 - k])

            act.wait_ge(rowsT_ready, 1)
            rows_high(R0, 0, 2, 0)
            act.wait_ge(step_tables, 2)
            step(R0, 0)
            step(R0 + 1, 1)
            with act.Fori(0, (R1 - 1 - UNROLLED) // 2) as g:
                for j in range(2):
                    step(2 * g + (UNROLLED + j), j)
            for t in range(R1 - 1, N + 2):
                step(t, t % 2)

        @block.tensor
        def _(pe):
            t_ = nc.tensor
            pe.wait_ge(const_ready, 1)

            def condition(i, k, xt, f):
                pe.wait_ge(bd_ready, PB * (i + 1))
                if f:
                    pe.wait_ge(h_ready, i - 3)
                t_.matmul(pC[k][:, :], bd[:, k, :], xt, start=True, stop=True).then_inc(cond_done, 1)

            def transpose_h(b, j, m, f):
                pe.wait_ge(h_ready, 2 * b + j + 1)
                if f and j == 0:
                    pe.wait_ge(logits_taken, b)
                if f and j == 1:
                    pe.wait_ge(odd_lo_ready, b)
                chunks = h[:, 2 * m + j, :].rearrange("p (d c) -> p c d", c=DC)
                for c in range(DC):
                    ins = t_.transpose(pH[j][:, c * P:(c + 1) * P], chunks[:, c, :], ident[:, :])
                ins.then_inc(hT_ready, 1)

            def route(b, m):
                pe.wait_ge(rlo_ready, b + 1)
                pe.wait_ge(odd_lo_ready, b + 1)
                for j, rowT in enumerate((rowsT[:, m], oddT)):
                    for c in range(DC):
                        for n, (u, w) in enumerate(PARTS):
                            ins = t_.matmul(pLogits[:, j * E:(j + 1) * E], rowT[:, u, c * P:(c + 1) * P], router16[:, w, c, :],
                                            start=(c == 0 and n == 0), stop=(c == DC - 1 and n == 2))
                ins.then_inc(routed, 1)

            def transpose_rows(t, k):
                pe.wait_ge(gathered[k], 8 * (t - k - R0) + 16)
                pe.wait_ge(rlo_ready, t - 1)
                chunks = rows[:, k, :].rearrange("p (d c) -> p c d", c=DC)
                for c in range(DC):
                    ins = t_.transpose(pH[k][:, c * P:(c + 1) * P], chunks[:, c, :], ident[:, :])
                ins.then_inc(rowsT_ready, 1)

            def step_expert(t):
                if isinstance(t, int) and (t < R0 or t >= R1):
                    return 0
                if isinstance(t, int) and t == R0:
                    pe.wait_ge(step_tables, 2)
                return pe.value_load(expert[0:1, bass.ds(t, 1)], min_val=0, max_val=E)

            def gate_up(t, k, e, bank, taken):
                if isinstance(t, int) and t >= R1:
                    pe.wait_ge(rows_loaded[(t - R1) % 4], 16 * ((t - R1) // 4 + 1))
                else:
                    pe.wait_ge(rlo_ready, t + 1)
                if taken is not None:
                    pe.wait_ge(a_ready, taken)
                rowT = last_T(t) if isinstance(t, int) and t >= R1 else rowsT[:, k]
                for c in range(DC):
                    for m, (u, w) in enumerate(PARTS):
                        ins = t_.matmul(pG[bank][:, :].rearrange("p (m f) -> p m f", m=2), rowT[:, u, c * P:(c + 1) * P],
                                        gu_chunk(W[:, e, w, 0:GU], c),
                                        start=(c == 0 and m == 0), stop=(c == DC - 1 and m == 2))
                ins.then_inc(gu_ready, 1)

            def transpose_a(t, k, bank, free):
                pe.wait_ge(as_ready, t + 1)
                if free is not None:
                    pe.wait_ge(*free)
                chunks = a_scaled[:, k, :].rearrange("p (f c) -> p c f", c=FC)
                for c in range(FC):
                    ins = t_.transpose(bank[:, c * P:(c + 1) * P], chunks[:, c, :], ident[:, :])
                ins.then_inc(aT_ready, 1)

            def down(t, k, e, bank, taken):
                pe.wait_ge(alo_ready, t + 1)
                if taken is not None:
                    pe.wait_ge(y_ready, taken)
                for c in range(FC):
                    for m, (u, w) in enumerate(PARTS):
                        ins = t_.matmul(bank[:, :], aT[:, k, u, c * P:(c + 1) * P], W[:, e, w, GU + c * D:GU + (c + 1) * D],
                                        start=(c == 0 and m == 0), stop=(c == FC - 1 and m == 2))
                ins.then_inc(down_ready, 1)

            def pair(b, m):
                for j in range(2):
                    transpose_h(b, j, m, b)
                if b == 1:
                    pe.wait_ge(gu_lo_ready, 1)
                if b >= 1:
                    gate_up(b - 1, 1 - m, 0, 0, b - 1 if b >= 2 else None)
                if b >= 2:
                    transpose_a(b - 2, m, pY[0], (y_ready, b - 2) if b >= 3 else None)
                if b + 2 < NP:
                    if b % 2 == 0 and b < 4:
                        pe.wait_ge(x_loaded[b // 2 + 1], 32)
                    condition(2 * b + 4, 2 * m, x_even[:, b + 2, :], 1)
                    condition(2 * b + 5, 2 * m + 1, x_odd[:, b + 2, :], 1)
                if b == 0:
                    pe.wait_ge(router_ready, 1)
                route(b, m)
                if b == 2:
                    pe.wait_ge(dn_lo_ready, 1)
                if b >= 2:
                    down(b - 2, m, 0, pY[0], None)

            pe.wait_ge(x_loaded[0], 32)
            for b in range(2):
                if b == 1:
                    pe.wait_ge(x_loaded[3], 32)
                condition(2 * b, 2 * b, x_even[:, b, :], 0)
                condition(2 * b + 1, 2 * b + 1, x_odd[:, b, :], 0)
            for b in range(NP):
                pair(b, b % 2)

            def ranks():
                pe.wait_ge(sel_ready, 1)
                pe.wait_ge(const_ready, 9)
                flat = sel[:, :, :].rearrange("p i e -> p (i e)")
                t_.matmul(pRank, before[:, :], flat, start=True, stop=False)
                for n in range(1, NT):
                    t_.matmul(pRank[:, n * E:], ones[:, :], flat[:, 0:(NT - n) * E], start=False, stop=(n == NT - 1))
                for n in range(NT):
                    ins = t_.matmul(pCount, ones[:, :], sel[:, n, :], start=(n == 0), stop=(n == NT - 1))
                ins.then_inc(rank_ready, 1)

            def invert():
                pe.wait_ge(row_hots_ready, 1)
                pe.wait_ge(step_hots_ready, TOP)
                pe.wait_ge(rank_taken, 1)
                for m in range(TOP * NT):
                    ins = t_.matmul(pRows, one_hot_row[:, m, :], one_hot_step[:, m, :], start=(m == 0), stop=(m == TOP * NT - 1))
                ins.then_inc(inverse_ready, 1)

            gate_up(R0 - 1, 1, 0, 0, R0 - 1)
            transpose_a(R0 - 2, 0, pY[0], (y_ready, R0 - 2))
            ranks()
            down(R0 - 2, 0, 0, pY[0], None)
            invert()
            transpose_a(R0 - 1, 1, pY[0], (y_ready, R0 - 1))
            down(R0 - 1, 1, 0, pY[0], None)

            def step(t, k):
                inside = isinstance(t, int)
                if not inside or t + 1 < R1:
                    transpose_rows(t + 1, 1 - k)
                if inside and t == R0:
                    pe.wait_ge(gu_lo_ready, NE)
                    pe.wait_ge(dn_lo_ready, NE)
                if not inside or t < N:
                    gate_up(t, k, step_expert(t), k, t if inside and t == R0 else t - 1)
                if not inside or t >= R0 + 2:
                    if inside and t == R0 + 3:
                        pe.wait_ge(rows_table, 1)
                    down(t - 2, k, step_expert(t - 2), pY[k], t - 2 if inside and t == R0 + 2 else t - 3)
                if not inside or (t > R0 and t <= N):
                    transpose_a(t - 1, 1 - k, pT[1 - k], (alo_ready, t - 2))

            pe.wait_ge(logits_taken, NP)
            transpose_rows(R0, 0)
            step(R0, 0)
            step(R0 + 1, 1)
            with pe.Fori(0, (R1 - 1 - UNROLLED) // 2) as g:
                for j in range(2):
                    step(2 * g + (UNROLLED + j), j)
            for t in range(R1 - 1, N + 2):
                step(t, t % 2)


_INS = ['x', 'itok_B_1_198', 'L0_cond_weights', 'L0_ffn_rms_weight', 'L0_ffn_router_w', 'L0_ffn_w_gate', 'L0_ffn_w_up',
        'L0_ffn_w_down', 'L0_ffn_sw_gate', 'L0_ffn_sw_up', 'L0_ffn_sw_down']


def kernel(**inputs):
    import numpy as _np
    import concourse.bacc as _bacc
    from concourse import mybir as _mybir
    from concourse.bass_utils import run_bass_kernel_spmd as _run

    nc = _bacc.Bacc("TRN2", target_bir_lowering=False, num_devices=1)
    arrays, args = {}, []
    for name in _INS:
        a = _np.ascontiguousarray(inputs[name])
        arrays[f"in_{name}_dram"] = a
        args.append(nc.dram_tensor(f"in_{name}_dram", a.shape, _mybir.dt.from_np(a.dtype), kind="ExternalInput").ap())
    shape = inputs['x'].shape
    args.append(nc.dram_tensor("out_dram", tuple(shape), _mybir.dt.float32, kind="ExternalOutput").ap())
    adaln_moe_kernel(nc, *args)
    r = _run(nc, [arrays], core_ids=[0])
    return r.results[0]["out_dram"]
```
